# Optimizing a Trainium2 kernel written in Bass

```python
import numpy as np
import jax
import jax.numpy as jnp

def _softmax(x, axis=-1):
    return jax.nn.softmax(x, axis=axis)

def _gelu(x):
    return jax.nn.gelu(x, approximate=True)

def _silu(x):
    return jax.nn.silu(x)

def _sigmoid(x):
    return jax.nn.sigmoid(x)

def _layernorm(x, axis=-1, eps=1e-05):
    m = jnp.mean(x, axis=axis, keepdims=True)
    v = jnp.var(x, axis=axis, keepdims=True)
    return (x - m) / jnp.sqrt(v + eps)

def _scatter_add(tgt, idx, src, axis=0):
    return tgt.at[idx].add(src)

def _segment_sum(src, seg, n):
    return jax.ops.segment_sum(src, seg, n)
kernel_name = 'mk_cond_resid_d2_seqx_r8_57bb48'

def setup_inputs(seed: int=0):
    np.random.seed(seed)
    _w = jnp.asarray

    def _rec_inputs():
        import jax
        import jax.numpy as jnp
        _rk = jax.random.key(seed)
        x = -0.0002071 + 1 * jax.random.normal(jax.random.fold_in(_rk, 1), (128, 32, 128), jnp.float32)
        _lenS = 32 - jax.random.randint(jax.random.fold_in(_rk, 7), (128,), 0, max(1, 32 // 4) + 1, jnp.int32)
        _lenS2 = 32 - jax.random.randint(jax.random.fold_in(_rk, 8), (128,), 0, max(1, 32 // 4) + 1, jnp.int32)
        cond_8 = jax.random.uniform(jax.random.fold_in(_rk, 11), (128, 8), jnp.float32, 0.0, 0.983423)
        return (x, cond_8)
    x, cond_8 = _rec_inputs()

    def _L0_cond_setup():
        import jax, jax.numpy as jnp
        import numpy as np
        R = 16
        ALPHA = 32.0
        SCALING = ALPHA / R
        key = jax.random.key(seed)
        ks = jax.random.split(key, 6)
        B, T, C, O, E = (16, 1500, 128, 128, 8)
        x = jax.random.normal(ks[0], (B, T, C), dtype=jnp.float32)
        w = jax.random.uniform(ks[1], (B, E), dtype=jnp.float32)
        W_base = jax.random.normal(ks[2], (O, C), dtype=jnp.float32) * 0.02
        b_base = jax.random.normal(ks[3], (O,), dtype=jnp.float32) * 0.02
        As = jax.random.normal(ks[4], (E, R, C), dtype=jnp.float32) * 0.02
        Bs = jax.random.normal(ks[5], (E, O, R), dtype=jnp.float32) * 0.02
        return {'x': x, 'w': w, 'W_base': W_base, 'b_base': b_base, 'As': As, 'Bs': Bs}
    _L0_cond_all = _L0_cond_setup()
    _L0_cond_in = {k: v for k, v in _L0_cond_all.items() if k in ('W_base', 'b_base', 'As', 'Bs')}
    del _L0_cond_all

    def _L1_cond_setup():
        import jax, jax.numpy as jnp
        import numpy as np
        TOP_K = 2
        NUM_MOE_LAYERS = 12

        def _gemma_mlp(x, gate_w, up_w, down_w):
            g = jnp.einsum('bsh,hi->bsi', x, gate_w)
            u = jnp.einsum('bsh,hi->bsi', x, up_w)
            return jnp.einsum('bsi,ih->bsh', jax.nn.gelu(g, approximate=True) * u, down_w)
        key = jax.random.key(seed)
        ks = jax.random.split(key, 8)
        B, S, H, I, E = (32, 32, 128, 512, 8)
        std = 0.02
        return {'x': jax.random.normal(ks[0], (B, S, H), jnp.float32), 'router_logits': jax.random.normal(ks[1], (B, E), jnp.float32), 'skill_gate': jax.random.normal(ks[2], (E, H, I), jnp.float32) * std, 'skill_up': jax.random.normal(ks[3], (E, H, I), jnp.float32) * std, 'skill_down': jax.random.normal(ks[4], (E, I, H), jnp.float32) * std, 'shared_gate': jax.random.normal(ks[5], (H, I), jnp.float32) * std, 'shared_up': jax.random.normal(ks[6], (H, I), jnp.float32) * std, 'shared_down': jax.random.normal(ks[7], (I, H), jnp.float32) * std}
    _L1_cond_all = _L1_cond_setup()
    _L1_cond_in = {k: v for k, v in _L1_cond_all.items() if k in ('skill_gate', 'skill_up', 'skill_down', 'shared_gate', 'shared_up', 'shared_down')}
    del _L1_cond_all
    return {'x': x, 'cond_8': cond_8, 'L0_cond_W_base': _L0_cond_in['W_base'], 'L0_cond_b_base': _L0_cond_in['b_base'], 'L0_cond_As': _L0_cond_in['As'], 'L0_cond_Bs': _L0_cond_in['Bs'], 'L1_cond_skill_gate': _L1_cond_in['skill_gate'], 'L1_cond_skill_up': _L1_cond_in['skill_up'], 'L1_cond_skill_down': _L1_cond_in['skill_down'], 'L1_cond_shared_gate': _L1_cond_in['shared_gate'], 'L1_cond_shared_up': _L1_cond_in['shared_up'], 'L1_cond_shared_down': _L1_cond_in['shared_down']}

def reference(x, cond_8, L0_cond_W_base, L0_cond_b_base, L0_cond_As, L0_cond_Bs, L1_cond_skill_gate, L1_cond_skill_up, L1_cond_skill_down, L1_cond_shared_gate, L1_cond_shared_up, L1_cond_shared_down):
    import jax
    import jax.numpy as jnp

    def _L0_cond_ref(x, w, W_base, b_base, As, Bs):
        import jax, jax.numpy as jnp
        import numpy as np
        R = 16
        ALPHA = 32.0
        SCALING = ALPHA / R
        out = jnp.einsum('btc,oc->bto', x, W_base) + b_base
        h = jnp.einsum('btc,erc->bter', x, As)
        lora = jnp.einsum('bter,eor,be->bto', h, Bs, w)
        return out + lora * SCALING

    def _L1_cond_ref(x, router_logits, skill_gate, skill_up, skill_down, shared_gate, shared_up, shared_down):
        import jax, jax.numpy as jnp
        import numpy as np
        TOP_K = 2
        NUM_MOE_LAYERS = 12

        def _gemma_mlp(x, gate_w, up_w, down_w):
            g = jnp.einsum('bsh,hi->bsi', x, gate_w)
            u = jnp.einsum('bsh,hi->bsi', x, up_w)
            return jnp.einsum('bsi,ih->bsh', jax.nn.gelu(g, approximate=True) * u, down_w)
        B = x.shape[0]
        E = skill_gate.shape[0]
        rw = jax.nn.softmax(router_logits.astype(jnp.float32), axis=-1)
        w, sel = jax.lax.top_k(rw, TOP_K)
        w = w / w.sum(axis=-1, keepdims=True)
        w = w.astype(x.dtype)
        scale = 1.0 / NUM_MOE_LAYERS
        w = scale * w + (1.0 - scale) * jax.lax.stop_gradient(w)
        dense_w = jnp.zeros((B, E), x.dtype).at[jnp.arange(B)[:, None], sel].add(w)

        def step(acc, params):
            g, u, d, we = params
            return (acc + we[:, None, None] * _gemma_mlp(x, g, u, d), None)
        out, _ = jax.lax.scan(step, jnp.zeros_like(x), (skill_gate, skill_up, skill_down, dense_w.T))
        out = out + _gemma_mlp(x, shared_gate, shared_up, shared_down)
        return out
    x = x + _L0_cond_ref(x, cond_8, L0_cond_W_base, L0_cond_b_base, L0_cond_As, L0_cond_Bs)
    x = x + _L1_cond_ref(x, cond_8, L1_cond_skill_gate, L1_cond_skill_up, L1_cond_skill_down, L1_cond_shared_gate, L1_cond_shared_up, L1_cond_shared_down)
    return x

_drawn_inputs = setup_inputs


def setup_inputs(seed=0):
    import zlib

    import numpy as np

    out = dict(_drawn_inputs(seed))
    spreads = {}
    factors = {'L0_cond_b_base': 2.833,
     'L1_cond_skill_gate': 6.463,
     'L1_cond_skill_up': 6.396,
     'L1_cond_skill_down': 6.392,
     'L1_cond_shared_gate': 4.607,
     'L1_cond_shared_up': 4.525,
     'L1_cond_shared_down': 4.523}
    for name, (base, spread) in spreads.items():
        noise = np.random.default_rng([zlib.crc32(name.encode()), seed]).standard_normal(out[name].shape)
        drawn = base * np.exp(spread * noise) if base else spread * noise
        out[name] = jnp.asarray(drawn.astype(out[name].dtype))
    for name, factor in factors.items():
        out[name] = (out[name] * factor).astype(out[name].dtype)
    return out
```

```python
from contextlib import ExitStack

import concourse.bass as bass
from concourse import mybir

ALU = mybir.AluOpType
ACT = mybir.ActivationFunctionType
AX = mybir.AxisListType
ET = mybir.EngineType
F16 = mybir.dt.float16
F32 = mybir.dt.float32
I32 = mybir.dt.int32
ABSMAX = bass.bass_isa.ReduceOp.absmax
ds = bass.ds

P = 128
EXPONENT_MASK = 0x7F800000
TINY = 2.0 ** -24
TOP = 14
MASKED = -3.0e38


def ceil_div(a, b):
    return -(-a // b)


class Stage:

    def __init__(self, sem, name, n, chunks, parity):
        self.n, self.parity = n, parity
        self.last_parity = (parity + n - 1) % 2
        self.gate_up = [sem(f"{name}_gate_up_{c}") for c in range(chunks)]
        self.gelu = [sem(f"{name}_gelu_{c}") for c in range(chunks)]
        self.hidden = [sem(f"{name}_hidden_{c}") for c in range(chunks)]
        self.hidden_hi = [sem(f"{name}_hidden_hi_{c}") for c in range(chunks)]
        self.hidden_lo = [sem(f"{name}_hidden_lo_{c}") for c in range(chunks)]
        self.down = sem(f"{name}_down")
        self.taken = sem(f"{name}_taken")


def lora_moe_kernel(nc, x, cond, w_base, b_base, lora_a, lora_b, skill_gate, skill_up, skill_down,
                    shared_gate, shared_up, shared_down, out):
    B, S, C = x.shape
    E, R, _ = lora_a.shape
    F = shared_gate.shape[1]
    LORA_SCALING = 32.0 / R
    MOE_SCALE = 1.0 / 12
    assert B == P and C == P and E * R == P and E == 8 and P % S == 0

    TILE = 512
    TB = TILE // S
    NT = B * S // TILE
    SUB = TILE // P
    QB = P // S
    CHUNKS = F // P
    XRING = 4
    FIRST = 5
    LATER = NT - FIRST
    GROUP = 12
    GW = GROUP * S
    GQ = GW // P
    BLOCKS = (2 * B + E * (GROUP - 1)) // GROUP
    SLOTS = BLOCKS * GROUP
    FILLS = ceil_div(B, GROUP)
    LAND = 2 * B
    WSTRIDE = 2 * F
    SHARED = E
    assert FIRST % 2 == 1 and LATER % 2 == 1 and NT % XRING == 0 and GW % P == 0

    with ExitStack() as ctx:
        def sb(name, shape, dt):
            return ctx.enter_context(nc.sbuf_tensor(name, shape, dt))

        def psum(name, shape):
            return ctx.enter_context(nc.psum_tensor(name, shape, F32))

        def sem(name):
            return ctx.enter_context(nc.semaphore(name))

        expert_out = nc.dram_tensor("expert_out", [SLOTS, S, C], F32, kind="Internal").ap()

        ps_gate = psum("ps_gate", [P, 2, TILE])
        ps_up = psum("ps_up", [P, 2, TILE])
        ps_down = psum("ps_down", [P, 2, TILE])
        ps_misc = psum("ps_misc", [P, 2, TILE])
        ps_xt, ps_lora, ps_x1 = ps_gate, ps_up, ps_down

        ident = sb("ident", [P, P], F32)
        adapter_rows = sb("adapter_rows", [E, P], F32)
        before_me = sb("before_me", [P, P], F32)
        ones = sb("ones", [P, P], F32)
        ones_h = sb("ones_h", [P, 1], F16)
        batch_m512 = sb("batch_m512", [P, 1], F16)
        b128_h = sb("b128_h", [P, 1], F16)
        rev = sb("rev", [P, E], F32)
        fills = sb("fills", [P, E, FILLS], F32)
        upto = sb("upto", [P, E, E], F32)
        quarter = sb("quarter", [P, QB], F32)
        block_slot = sb("block_slot", [1, BLOCKS, E - 1], F32)

        cond_sb = sb("cond_sb", [P, E], F32)
        bias = sb("bias", [P, 1], F32)
        small_t = sb("small_t", [P, 3, P], F32)
        cond_t = sb("cond_t", [E, P], F32)
        lora_w = sb("lora_w", [P, B], F32)
        ring = sb("ring", [P, XRING, SUB, C], F32)
        pair = sb("pair", [P, 2, TILE], F32)
        x1t = sb("x1t", [P, B * S], F32)
        x1s = sb("x1s", [P, B, 2, S], F16)
        w32 = sb("w32", [P, 3, E + 1, F], F32)
        w16 = sb("w16", [P, 3, (E + 1) * WSTRIDE], F16)
        base = sb("base", [P, FIRST, TILE], F32)

        gate_e = sb("gate_e", [P, E], F32)
        choice = sb("choice", [P, 2, E], F32)
        tmp_e = sb("tmp_e", [P, 4, E], F32)
        tmp_c = sb("tmp_c", [P, 16], F32)
        chosen = sb("chosen", [P, E], F32)
        tmp_fill = sb("tmp_fill", [P, E, FILLS], F32)
        tmp_ee = sb("tmp_ee", [P, E, E], F32)
        n_blocks = sb("n_blocks", [P, E], F32)
        ends = sb("ends", [P, E], F32)
        place = sb("place", [P, E], F32)
        pos = sb("pos", [P, 2], F32)
        w_col = sb("w_col", [P, 2, P], F32)
        taken_h = sb("taken_h", [P, SLOTS], F16)
        second_h = sb("second_h", [P, SLOTS], F16)
        below_h = sb("below_h", [P, 2, SLOTS], F16)
        dst_i = sb("dst_i", [1, SLOTS], I32)
        src_i = sb("src_i", [1, SLOTS], I32)
        exp_f = sb("exp_f", [1, BLOCKS], F32)
        exp_i = sb("exp_i", [1, BLOCKS], I32)
        slot_w = sb("slot_w", [P, BLOCKS * GQ], F32)

        peak = sb("peak", [P, 2, 4], F32)
        peak_all = sb("peak_all", [P, 2, 4], F32)
        tile_peak = sb("tile_peak", [P, NT], F32)
        p2 = sb("p2", [P, 2, 4], F32)
        ip2 = sb("ip2", [P, 2, 4], F32)
        scale = sb("scale", [P, 2, 4], F32)
        work = sb("work", [P, 2, 6], F32)
        g_scale = sb("g_scale", [P, 2], F32)
        u_scale = sb("u_scale", [P, 2], F32)
        y_scale = sb("y_scale", [P, 2], F32)
        y_unit = sb("y_unit", [P, 2], F32)

        act_g = sb("act_g", [P, 2, TILE], F32)
        hid = sb("hid", [P, 2, TILE], F32)
        hid_hi = sb("hid_hi", [P, 2, CHUNKS, TILE], F16)
        hid_lo = sb("hid_lo", [P, 2, CHUNKS, TILE], F16)
        gathered = sb("gathered", [P, 2, GROUP, 2, S], F16)
        y_sb = sb("y_sb", [P, 2, GQ, C], F32)

        slot1 = hid[:, 0, 0:SLOTS]
        slot2 = hid[:, 1, 0:SLOTS]
        x_scaled = y_sb[:].rearrange("p j q c -> p (j q c)")[:, 0:TILE]
        wb_sb, la_sb, lb_sb = (base[:, 2, i * P:i * P + P] for i in range(3))
        xt, mixed = pair, base[:, 0:2]
        x1_unit = pair
        slot_id = act_g[:, 0, 0:SLOTS]
        land_id = act_g[0:1, 1, 0:SLOTS]
        spare = ring[:].rearrange("p t q c -> p (t q c)")
        row_z, row_a, row_c = (spare[0:1, i * SLOTS:(i + 1) * SLOTS] for i in range(3))
        w_slot = spare[:, 3 * SLOTS:4 * SLOTS]
        cmp_b = spare[0:1, 4 * SLOTS:4 * SLOTS + BLOCKS * (E - 1)].rearrange(
            "p (k e) -> p k e", e=E - 1)

        cond_in, small_in = sem("cond_in"), sem("small_in")
        x_in = [sem(f"x_in_{i}") for i in range(XRING)]
        shared_in = sem("shared_in")
        gate_in, up_in, down_in = sem("gate_in"), sem("up_in"), sem("down_in")
        consts, consts2 = sem("consts"), sem("consts2")
        pool_chain, dve_chain, act_chain = sem("pool_chain"), sem("dve_chain"), sem("act_chain")
        small_tr, small_out, lora_w_ps, lora_w_ready = (
            sem("small_tr"), sem("small_out"), sem("lora_w_ps"), sem("lora_w_ready"))
        neg_max, exped, chosen_ready, ranks, pos_ready, w_col_ready = (
            sem("neg_max"), sem("exped"), sem("chosen_ready"), sem("ranks"), sem("pos_ready"),
            sem("w_col_ready"))
        maps_ready, rows_ps, rows_out, routed = (
            sem("maps_ready"), sem("rows_ps"), sem("rows_out"), sem("routed"))
        xt_ps, xt_out, lora_ps, lora_mixed, x1_ps, x1_out = (
            sem("xt_ps"), sem("xt_out"), sem("lora_ps"), sem("lora_mixed"), sem("x1_ps"),
            sem("x1_out"))
        peaks_a, peaks_b, peaks_all_a, peaks_all_b, scale_a, scale_b = (
            sem("peaks_a"), sem("peaks_b"), sem("peaks_all_a"), sem("peaks_all_b"),
            sem("scale_a"), sem("scale_b"))
        down_squares = sem("down_squares")
        x1_hi, x1_lo = sem("x1_hi"), sem("x1_lo")
        ws_hi, ws_lo, we_hi, we_lo = sem("ws_hi"), sem("ws_lo"), sem("we_hi"), sem("we_lo")
        x1_unit_a, x1_unit_c = sem("x1_unit_a"), sem("x1_unit_c")
        slots_in, scattered = sem("slots_in"), [sem("scattered_0"), sem("scattered_1")]
        back_in = [sem("back_in_0"), sem("back_in_1")]
        back_sum, base_sum, stored = sem("back_sum"), sem("base_sum"), sem("stored")
        stage_a = Stage(sem, "first", FIRST, CHUNKS, 0)
        stage_b = Stage(sem, "block", BLOCKS, CHUNKS, (stage_a.last_parity + 1) % 2)
        stage_c = Stage(sem, "later", LATER, CHUNKS, (stage_b.last_parity + 1) % 2)

        x_dram = x.rearrange("b s c -> (b s) c").rearrange("(t q p) c -> t p q c", q=SUB, p=P)
        out_dram = out.rearrange("b s c -> (b s) c").rearrange("(t q p) c -> t p q c", q=SUB, p=P)
        rows_dram = expert_out[0:2 * B].rearrange("r s c -> (r s) c").rearrange(
            "(t q p) c -> t p q c", q=SUB, p=P)

        def values(engine, ap, least, most):
            _, v = nc.values_load_multi_w_load_instructions(
                ap, engines=[engine], min_val=least, max_val=most,
                skip_runtime_bounds_check_because="the routing gives values in these bounds")
            return v

        def steps(e, n, step):
            step(0, 0)
            with e.Fori(1, n - 1 if n % 2 else n - 2, 2) as k:
                step(k, 1)
                step(k + 1, 0)
            if n % 2 == 0:
                step(n - 1, 1)

        def share(n, i, of):
            return range(n * i // of, n * (i + 1) // of)

        block = ctx.enter_context(nc.Block())

        @block.sync
        def _(sp):
            sp.dma_start(cond_sb[:], cond).then_inc(cond_in, 16)
            sp.dma_start(wb_sb, w_base).then_inc(small_in, 16)
            sp.dma_start(la_sb, lora_a.rearrange("e r c -> (e r) c")).then_inc(small_in, 16)
            sp.dma_start(lb_sb.rearrange("o (e r) -> o e r", e=E), lora_b.rearrange("e o r -> o e r")).then_inc(small_in, 16)
            sp.dma_start(bias[:], b_base.rearrange("(o u) -> o u", u=1)).then_inc(small_in, 16)
            for r in range(XRING):
                sp.dma_start(ring[:, r], x_dram[r]).then_inc(x_in[r], 16)
            with sp.Fori(XRING, NT - XRING + 1, XRING) as t:
                for r in range(XRING):
                    sp.wait_ge(xt_ps, t - XRING + r + 1)
                    sp.dma_start(ring[:, r], x_dram[ds(t + r, 1)].rearrange("u p q c -> p (u q) c")
                                 ).then_inc(x_in[r], 16)

            sp.wait_ge(routed, 1)

            def scatter(k, j):
                for a in range(0, GROUP, QB):
                    rows = values(ET.SP, dst_i[0:1, ds(k * GROUP + a, QB)], 0, SLOTS - 1)
                    if a == 0:
                        sp.wait_ge(stage_b.taken, k + 1)
                    for i in range(QB):
                        sp.dma_start(
                            expert_out[ds(rows[i], 1)].rearrange("u s c -> (u s) c"),
                            y_sb[S * i:S * i + S, j, a // QB]).then_inc(scattered[j], 16)
            steps(sp, BLOCKS, scatter)

            for j in range(2):
                sp.wait_ge(scattered[j], 16 * BLOCKS // 2 * GROUP)

            def fetch(t, j):
                if 2 <= t < FIRST + 2:
                    sp.wait_ge(base_sum, t - 1)
                elif t >= 2:
                    sp.wait_ge(stored, 16 * (t - 1))
                for h in range(2):
                    sp.dma_start(ring[:, 2 * j + h],
                                 rows_dram[h * NT + t]
                                 ).then_inc(back_in[j], 16)

            fetch(0, 0)
            fetch(1, 1)
            for t in range(NT):
                if t < FIRST:
                    sp.wait_ge(base_sum, t + 1)
                    sp.dma_start(out_dram[t], base[:, t].rearrange("p (q c) -> p q c", q=SUB)
                                 ).then_inc(stored, 16)
                else:
                    sp.wait_ge(stage_c.taken, t - FIRST + 1)
                    sp.dma_start(out_dram[t], ring[:, 2 * (t % 2)]).then_inc(stored, 16)
                if t + 2 < NT:
                    fetch(t + 2, t % 2)
            sp.wait_ge(stored, 16 * NT)

        @block.tensor
        def _(pe):
            pe.wait_ge(consts, 1)
            pe.wait_ge(small_in, 64)
            pe.wait_ge(cond_in, 16)
            pe.transpose(ps_misc[:, 0, 0:P], wb_sb, ident[:])
            pe.transpose(ps_misc[:, 0, P:2 * P], la_sb, ident[:])
            pe.transpose(ps_misc[:, 0, 2 * P:3 * P], lb_sb, ident[:])
            pe.transpose(ps_misc[0:E, 0, 3 * P:4 * P], cond_sb[:], ident[:]).then_inc(small_tr, 1)
            pe.wait_ge(small_out, 1)
            pe.matmul(ps_misc[:, 1, 0:B], adapter_rows[:], cond_t[:], start=True, stop=True
                      ).then_inc(lora_w_ps, 1)
            pe.wait_ge(chosen_ready, 1)
            pe.wait_ge(consts2, 1)
            pe.wait_ge(lora_w_ready, 1)
            pe.matmul(ps_misc[:, 1, 0:E], before_me[:], chosen[:], start=True, stop=True)
            pe.matmul(ps_misc[:, 1, E:2 * E], ones[:], chosen[:], start=True, stop=True
                      ).then_inc(ranks, 1)

            def turn(t, r, in_flight):
                pe.wait_ge(x_in[r], in_flight)
                if not isinstance(t, int) or t >= 2:
                    pe.wait_ge(xt_out, t - 1)
                for q in range(SUB):
                    mm = pe.transpose(ps_xt[:, r % 2, q * P:q * P + P], ring[:, r, q], ident[:])
                mm.then_inc(xt_ps, 1)

            def products(t, r):
                pe.wait_ge(xt_out, t + 1)
                if not isinstance(t, int) or t >= 2:
                    pe.wait_ge(x1_out, t - 1)
                pe.matmul(ps_lora[:, r % 2], small_t[:, 1], xt[:, r % 2], start=True, stop=True
                          ).then_inc(lora_ps, 1)
                pe.matmul(ps_x1[:, r % 2], small_t[:, 0], xt[:, r % 2], start=True, stop=False)

            def adapters(t, r):
                pe.wait_ge(lora_mixed, t + 1)
                pe.matmul(ps_x1[:, r % 2], small_t[:, 2], mixed[:, r % 2], start=False, stop=True
                          ).then_inc(x1_ps, 1)

            turn(0, 0, 16)
            for t in range(XRING - 1):
                products(t, t)
                turn(t + 1, t + 1, 16)
                adapters(t, t)
            with pe.Fori(XRING, NT - XRING + 1, XRING) as t:
                for r in range(XRING):
                    products(t + (r - 1), (r - 1) % XRING)
                    turn(t + r, r, 4 * (t + XRING))
                    adapters(t + (r - 1), (r - 1) % XRING)
            products(NT - 1, XRING - 1)
            adapters(NT - 1, XRING - 1)

            pe.wait_ge(maps_ready, 1)
            pe.wait_ge(pos_ready, 1)
            pe.wait_ge(w_col_ready, 1)
            pe.matmul(ps_misc[0:1, 0, 0:SLOTS], batch_m512[:], taken_h[:], start=True, stop=False)
            pe.matmul(ps_misc[0:1, 0, 0:SLOTS], b128_h[:], second_h[:], start=False, stop=True)
            pe.matmul(ps_misc[0:1, 1, 0:SLOTS], ones_h[:], below_h[:, 0], start=True, stop=True)
            pe.wait_ge(x1_out, NT)
            pe.matmul(ps_down[:, 1, 0:SLOTS], w_col[:, 0], slot1, start=True, stop=False)
            pe.matmul(ps_down[:, 1, 0:SLOTS], w_col[:, 1], slot2, start=False, stop=True
                      ).then_inc(rows_ps, 1)

            def gate_up(st, prev, k, c, weights, moving):
                first = isinstance(k, int) and k == 0
                if c >= 2:
                    pe.wait_ge(st.hidden[c - 2], k + 1)
                elif not first:
                    pe.wait_ge(st.hidden[CHUNKS + c - 2], k)
                elif prev is not None:
                    pe.wait_ge(prev.hidden[CHUNKS + c - 2], prev.n)
                x_hi, x_lo, width = moving
                for kind, bank in ((0, ps_gate), (1, ps_up)):
                    w_hi, w_lo = weights(kind, c * P), weights(kind, F + c * P)
                    o = bank[:, c % 2, 0:width]
                    pe.matmul(o, w_hi, x_hi, start=True, stop=False)
                    pe.matmul(o, w_hi, x_lo, start=False, stop=False)
                    mm = pe.matmul(o, w_lo, x_hi, start=False, stop=True)
                mm.then_inc(st.gate_up[c], 1)

            def down(st, k, par, subs, weights, with_x1, last_sub):
                if 0 in subs:
                    for c in range(CHUNKS):
                        pe.wait_ge(st.hidden_hi[c], k + 1)
                        pe.wait_ge(st.hidden_lo[c], k + 1)
                    if with_x1 is not None:
                        pe.wait_ge(with_x1, k + 1)
                for q in subs:
                    o = ps_down[:, par, q * P:q * P + P]
                    for c in range(CHUNKS):
                        h_hi = hid_hi[:, par, c, q * P:q * P + P]
                        h_lo = hid_lo[:, par, c, q * P:q * P + P]
                        w_hi, w_lo = weights(2, c * P), weights(2, F + c * P)
                        pe.matmul(o, h_hi, w_hi, start=(c == 0), stop=False)
                        pe.matmul(o, h_hi, w_lo, start=False, stop=False)
                        mm = pe.matmul(o, h_lo, w_hi, start=False,
                                       stop=(c == CHUNKS - 1 and with_x1 is None))
                    if with_x1 is not None:
                        mm = pe.matmul(o, x1_unit[:, par, q * P:q * P + P], ident[:],
                                       start=False, stop=True)
                if last_sub in subs:
                    mm.then_inc(st.down, 1)

            def shared_weights(kind, at):
                a = SHARED * WSTRIDE + at
                return w16[:, kind, a:a + P]

            def expert_weights(offset):
                return lambda kind, at: w16[:, kind, at:][:, ds(offset, P)]

            def tile_moving(t):
                xs = x1s[:, ds(t * TB, TB)]
                return xs[:, :, 0], xs[:, :, 1], TILE

            def block_moving(par):
                return gathered[:, par, :, 0], gathered[:, par, :, 1], GW

            def shared_down(st, k, par, subs, with_x1):
                down(st, k, par, subs, shared_weights, with_x1, SUB - 1)

            def block_down(k, par, subs, offset):
                st = stage_b
                weights = expert_weights(offset)
                for c in range(CHUNKS):
                    pe.wait_ge(st.hidden_hi[c], k + 1)
                    pe.wait_ge(st.hidden_lo[c], k + 1)
                    w_hi = weights(2, c * P)
                    for q in subs:
                        o = ps_down[:, par, q * P:q * P + P]
                        pe.matmul(o, hid_hi[:, par, c, q * P:q * P + P], w_hi,
                                  start=(c == 0 and q == 0), stop=False, skip_group_check=True)
                        pe.matmul(o, hid_lo[:, par, c, q * P:q * P + P], w_hi,
                                  start=False, stop=False, skip_group_check=True)
                    w_lo = weights(2, F + c * P)
                    for q in subs:
                        mm = pe.matmul(ps_down[:, par, q * P:q * P + P],
                                       hid_hi[:, par, c, q * P:q * P + P], w_lo, start=False,
                                       stop=(c == CHUNKS - 1), skip_group_check=True)
                mm.then_inc(st.down, 1)

            pe.wait_ge(ws_hi, 3)
            pe.wait_ge(ws_lo, 3)

            def first_tile(k, j):
                par = (stage_a.parity + j) % 2
                pe.wait_ge(x1_hi, k + 1)
                pe.wait_ge(x1_lo, k + 1)
                m = tile_moving(k)
                for c in range(CHUNKS):
                    gate_up(stage_a, None, k, c, shared_weights, m)
                    if c in (1, 2) and not (isinstance(k, int) and k == 0):
                        subs = range(SUB // 2) if c == 1 else range(SUB // 2, SUB)
                        shared_down(stage_a, k - 1, 1 - par, subs, x1_unit_a)
                if isinstance(k, int):
                    pe.wait_ge(rows_out, 1)
            steps(pe, FIRST, first_tile)

            pe.wait_ge(we_hi, 3 * E)
            pe.wait_ge(we_lo, 3 * E)
            pe.wait_ge(routed, 1)

            def expert_block(k, j):
                par = (stage_b.parity + j) % 2
                first = isinstance(k, int) and k == 0
                if first:
                    now = values(ET.PE, exp_i[0:1, 0:1], 0, (E - 1) * WSTRIDE)[0]
                else:
                    last, now = values(ET.PE, exp_i[0:1, ds(k - 1, 2)], 0, (E - 1) * WSTRIDE)
                pe.wait_ge(slots_in, k + 1)
                m = block_moving(par)
                for c in range(CHUNKS):
                    gate_up(stage_b, stage_a, k, c, expert_weights(now), m)
                    if first and c in (1, 2):
                        subs = range(SUB // 2) if c == 1 else range(SUB // 2, SUB)
                        shared_down(stage_a, FIRST - 1, 1 - par, subs, x1_unit_a)
                    if not first and c == 2:
                        block_down(k - 1, 1 - par, range(GQ), last)
            steps(pe, BLOCKS, expert_block)

            def later_tile(k, j):
                par = (stage_c.parity + j) % 2
                m = tile_moving(k + FIRST)
                first = isinstance(k, int) and k == 0
                if first:
                    last = values(ET.PE, exp_i[0:1, BLOCKS - 1:BLOCKS], 0, (E - 1) * WSTRIDE)[0]
                for c in range(CHUNKS):
                    gate_up(stage_c, stage_b, k, c, shared_weights, m)
                    if first and c == 2:
                        block_down(BLOCKS - 1, 1 - par, range(GQ), last)
                    if not first and c in (1, 2):
                        subs = range(SUB // 2) if c == 1 else range(SUB // 2, SUB)
                        shared_down(stage_c, k - 1, 1 - par, subs, x1_unit_c)
            steps(pe, LATER, later_tile)
            shared_down(stage_c, LATER - 1, stage_c.last_parity, range(SUB), x1_unit_c)

        @block.scalar
        def _(act):
            act.dma_start(w32[:, 0, SHARED], shared_gate).then_inc(shared_in, 16)
            act.dma_start(w32[:, 1, SHARED], shared_up).then_inc(shared_in, 16)
            act.dma_start(w32[:, 2, SHARED].rearrange("p (c h) -> p c h", c=CHUNKS),
                          shared_down.rearrange("(c p) h -> p c h", p=P)).then_inc(shared_in, 16)
            act.dma_start(w32[:, 2, 0:E].rearrange("p e (c h) -> p (e c) h", c=CHUNKS),
                          skill_down.rearrange("e (c p) h -> p (e c) h", p=P)).then_inc(down_in, 16)
            act.dma_start(w32[:, 0, 0:E], skill_gate.rearrange("e h i -> h e i")).then_inc(gate_in, 16)
            act.dma_start(w32[:, 1, 0:E], skill_up.rearrange("e h i -> h e i")).then_inc(up_in, 16)
            act.wait_ge(neg_max, 1)
            nc.scalar.activation(gate_e[:], cond_sb[:], ACT.Exp, bias=tmp_c[:, 1:2]).then_inc(exped, 1)
            act.wait_ge(small_tr, 1)
            nc.scalar.activation(small_t[:].rearrange("p a b -> p (a b)"), ps_misc[:, 0, 0:3 * P], ACT.Copy)
            nc.scalar.activation(cond_t[:], ps_misc[0:E, 0, 3 * P:4 * P], ACT.Copy).then_inc(small_out, 1)

            def copy_xt(t, j):
                act.wait_ge(xt_ps, t + 1)
                if not isinstance(t, int) or t >= 2:
                    act.wait_ge(x1_out, t - 1)
                nc.scalar.activation(xt[:, j], ps_xt[:, j], ACT.Copy).then_inc(xt_out, 1)
            steps(act, NT, copy_xt)
            act.wait_ge(down_in, 16)
            nc.scalar.activation(w16[:, 2, 0:E * F], w32[:, 2, 0:E].rearrange("p e f -> p (e f)"),
                                 ACT.Square, accum_out=tmp_c[:, 15:16]).then_inc(down_squares, 1)

            def split_hi(dst, src, s, done):
                nc.scalar.activation(dst, src, ACT.Copy, scale=s).then_inc(done, 1)

            def x_hi(t):
                split_hi(x1s[:, ds(t * TB, TB), 0], x1t[:, ds(t * TILE, TILE)].rearrange(
                    "p (b s) -> p b s", s=S), scale[:, 0, 0:1], x1_hi)

            def w_hi(kind, e, which, done):
                split_hi(w16[:, kind, ds(e * WSTRIDE, F)], w32[:, kind, ds(e, 1)].rearrange(
                    "p u f -> p (u f)"), scale[:, which, kind + 1:kind + 2], done)

            act.wait_ge(scale_a, 1)
            w_hi(0, SHARED, 0, ws_hi)
            x_hi(0)
            w_hi(1, SHARED, 0, ws_hi)
            w_hi(2, SHARED, 0, ws_hi)

            def gelu(st, prev, k, c, width, which):
                act.wait_ge(st.gate_up[c], k + 1)
                first = isinstance(k, int) and k == 0
                if c >= 2:
                    act.wait_ge(st.hidden[c - 2], k + 1)
                elif not first:
                    act.wait_ge(st.hidden[CHUNKS + c - 2], k)
                elif prev is not None:
                    act.wait_ge(prev.hidden[CHUNKS + c - 2], prev.n)
                nc.scalar.activation(act_g[:, c % 2, 0:width], ps_gate[:, c % 2, 0:width],
                                     ACT.Gelu_apprx_tanh, scale=g_scale[:, which:which + 1]
                                     ).then_inc(st.gelu[c], 1)

            def hidden_hi(st, prev, k, c, par, width):
                act.wait_ge(st.hidden[c], k + 1)
                if c == 0:
                    if not isinstance(k, int) or k >= 2:
                        act.wait_ge(st.down, k - 1)
                    elif k == 0 and prev is not None:
                        act.wait_ge(prev.down, prev.n - 1)
                nc.scalar.activation(hid_hi[:, par, c, 0:width], hid[:, c % 2, 0:width], ACT.Copy
                                     ).then_inc(st.hidden_hi[c], 1)

            def units(st, prev, k, j, width, which):
                par = (st.parity + j) % 2
                for c in range(CHUNKS):
                    gelu(st, prev, k, c, width, which)
                    if c >= 1:
                        hidden_hi(st, prev, k, c - 1, par, width)
                hidden_hi(st, prev, k, CHUNKS - 1, par, width)

            def x1_in_units(st, prev, k, par, t, done):
                if not isinstance(k, int) or k >= 2:
                    act.wait_ge(st.down, k - 1)
                nc.scalar.activation(x1_unit[:, par], x1t[:, ds(t * TILE, TILE)], ACT.Copy,
                                     scale=y_unit[:, 0:1]).then_inc(done, 1)

            def first_tile_start(k, j):
                units(stage_a, None, k, j, TILE, 0)
                x1_in_units(stage_a, None, k, (stage_a.parity + j) % 2, k, x1_unit_a)

            x_hi(1)
            x_hi(2)
            for k in range(FIRST):
                first_tile_start(k, k % 2)
                x_hi(k + NT - FIRST)
                if k == 2:
                    act.wait_ge(scale_b, 1)
                    act.wait_ge(down_squares, 1)
                if k >= 2:
                    for n in share(3 * E, k - 2, FIRST - 2):
                        w_hi(n % 3, n // 3, 1, we_hi)

            steps(act, BLOCKS, lambda k, j: units(stage_b, stage_a, k, j, GW, 1))

            def later_tile(k, j):
                units(stage_c, stage_b, k, j, TILE, 0)
                x1_in_units(stage_c, stage_b, k, (stage_c.parity + j) % 2, k + FIRST, x1_unit_c)
            steps(act, LATER, later_tile)

        @block.vector
        def _(dve):
            v = nc.vector
            chain = [0]

            def link(ins):
                chain[0] += 1
                ins.then_inc(dve_chain, 1)
                dve.wait_ge(dve_chain, chain[0])

            dve.wait_ge(cond_in, 16)
            link(v.tensor_reduce(tmp_c[:, 0:1], cond_sb[:], AX.X, ALU.max))
            v.tensor_scalar(tmp_c[:, 1:2], tmp_c[:, 0:1], -1.0, None, ALU.mult).then_inc(neg_max, 1)
            dve.wait_ge(consts, 2)
            link(v.scalar_tensor_tensor(tmp_e[:, 0], cond_sb[:], tmp_c[:, 0:1], rev[:], ALU.is_equal,
                                        ALU.mult))
            link(v.tensor_reduce(tmp_c[:, 2:3], tmp_e[:, 0], AX.X, ALU.max))
            link(v.tensor_scalar(choice[:, 0], rev[:], tmp_c[:, 2:3], None, ALU.is_equal))
            link(v.scalar_tensor_tensor(tmp_e[:, 1], choice[:, 0], MASKED, cond_sb[:], ALU.mult,
                                        ALU.add))
            link(v.tensor_reduce(tmp_c[:, 3:4], tmp_e[:, 1], AX.X, ALU.max))
            link(v.scalar_tensor_tensor(tmp_e[:, 0], tmp_e[:, 1], tmp_c[:, 3:4], rev[:],
                                        ALU.is_equal, ALU.mult))
            link(v.tensor_reduce(tmp_c[:, 4:5], tmp_e[:, 0], AX.X, ALU.max))
            link(v.tensor_scalar(choice[:, 1], rev[:], tmp_c[:, 4:5], None, ALU.is_equal))
            v.tensor_tensor(chosen[:], choice[:, 0], choice[:, 1], ALU.add).then_inc(chosen_ready, 1)
            dve.wait_ge(exped, 1)
            link(v.tensor_reduce(tmp_c[:, 5:6], gate_e[:], AX.X, ALU.add))
            link(v.reciprocal(tmp_c[:, 6:7], tmp_c[:, 5:6]))
            link(v.tensor_scalar(tmp_e[:, 2], gate_e[:], tmp_c[:, 6:7], None, ALU.mult))
            link(v.tensor_tensor(tmp_e[:, 0:2], choice[:], tmp_e[:, 2:3].broadcast_to([P, 2, E]), ALU.mult))
            link(v.tensor_reduce(tmp_c[:, 7:9], tmp_e[:, 0:2], AX.X, ALU.add))
            link(v.tensor_reduce(tmp_c[:, 9:10], tmp_c[:, 7:9], AX.X, ALU.add))
            link(v.reciprocal(tmp_c[:, 10:11], tmp_c[:, 9:10]))
            link(v.tensor_scalar(tmp_c[:, 11:13], tmp_c[:, 7:9], tmp_c[:, 10:11], None, ALU.mult))
            link(v.tensor_scalar(tmp_c[:, 13:15], tmp_c[:, 11:13], MOE_SCALE, None, ALU.mult))
            link(v.scalar_tensor_tensor(tmp_c[:, 7:9], tmp_c[:, 11:13], 1.0 - MOE_SCALE,
                                        tmp_c[:, 13:15], ALU.mult, ALU.add))
            v.tensor_scalar(w_col[:, 0], ones[:], tmp_c[:, 7:8], None, ALU.mult)
            v.tensor_scalar(w_col[:, 1], ones[:], tmp_c[:, 8:9], None, ALU.mult).then_inc(w_col_ready, 1)
            dve.wait_ge(lora_w_ps, 1)
            v.tensor_scalar(lora_w[:], ps_misc[:, 1, 0:B], LORA_SCALING, None, ALU.mult
                            ).then_inc(lora_w_ready, 1)
            dve.wait_ge(ranks, 1)
            link(v.tensor_copy(tmp_e[:, 0:2].rearrange("p a e -> p (a e)"), ps_misc[:, 1, 0:2 * E]))
            link(v.tensor_tensor(tmp_fill[:], tmp_e[:, 1].rearrange("p (e u) -> p e u", u=1)
                                 .broadcast_to([P, E, FILLS]), fills[:], ALU.is_gt))
            link(v.tensor_reduce(n_blocks[:], tmp_fill[:], AX.X, ALU.add))
            link(v.tensor_tensor(tmp_ee[:], n_blocks[:].rearrange("p (u e) -> p u e", u=1)
                                 .broadcast_to([P, E, E]), upto[:], ALU.mult))
            link(v.tensor_reduce(ends[:], tmp_ee[:], AX.X, ALU.add))
            link(v.scalar_tensor_tensor(tmp_e[:, 2], n_blocks[:], -float(GROUP), ends[:], ALU.mult,
                                        ALU.add))
            link(v.tensor_tensor(place[:], tmp_e[:, 0], tmp_e[:, 2], ALU.add))
            link(v.tensor_tensor(tmp_e[:, 0:2], choice[:], place[:].rearrange("p (u e) -> p u e", u=1)
                                 .broadcast_to([P, 2, E]), ALU.mult))
            v.tensor_reduce(pos[:], tmp_e[:, 0:2], AX.X, ALU.add).then_inc(pos_ready, 1)

            dve.wait_ge(lora_w_ready, 1)

            def layer0(t, j):
                tok = ds(t * TILE, TILE)
                dve.wait_ge(lora_ps, t + 1)
                if not isinstance(t, int) or t >= 2:
                    dve.wait_ge(x1_ps, t - 1)
                v.tensor_tensor(mixed[:, j].rearrange("p (b s) -> p b s", s=S),
                                ps_lora[:, j].rearrange("p (b s) -> p b s", s=S),
                                lora_w[:, ds(t * TB, TB)].rearrange("p (b u) -> p b u", u=1)
                                .broadcast_to([P, TB, S]), ALU.mult).then_inc(lora_mixed, 1)
                dve.wait_ge(x1_ps, t + 1)
                v.scalar_tensor_tensor(x1t[:, tok], ps_x1[:, j], bias[:, 0:1], xt[:, j], ALU.add,
                                       ALU.add).then_inc(x1_out, 1)
                dve.wait_ge(x1_out, t + 1)
                v.tensor_reduce(tile_peak[:, ds(t, 1)], x1t[:, tok], AX.X, ALU.max,
                                apply_absolute_value=True).then_inc(peaks_a, 1)
            dve.wait_ge(small_in, 64)
            steps(dve, NT, layer0)
            dve.wait_ge(shared_in, 48)
            v.tensor_reduce(peak[:, 0, 1:4], w32[:, :, SHARED], AX.X, ALU.max,
                            apply_absolute_value=True).then_inc(peaks_a, 1)
            dve.wait_ge(peaks_a, NT + 1)
            v.tensor_reduce(peak[:, 0, 0:1], tile_peak[:], AX.X, ALU.max).then_inc(peaks_a, 1)
            dve.wait_ge(rows_ps, 1)
            dve.wait_ge(maps_ready, 1)
            v.tensor_copy(row_z, ps_misc[0:1, 0, 0:SLOTS])
            v.scalar_tensor_tensor(row_a, ps_misc[0:1, 1, 0:SLOTS], -1.0, land_id, ALU.mult, ALU.add)
            v.tensor_copy(w_slot, ps_down[:, 1, 0:SLOTS]).then_inc(rows_out, 1)

            def scales(which, done):
                pk, pw, ip, sc, wk = (a[:, which] for a in (peak_all, p2, ip2, scale, work))
                link(v.tensor_scalar(pk, pk, TINY, None, ALU.max))
                link(v.tensor_scalar(pw.bitcast(I32), pk.bitcast(I32), EXPONENT_MASK, None,
                                     ALU.bitwise_and))
                link(v.reciprocal(ip, pw))
                v.tensor_scalar(sc, ip, 2.0 ** TOP, None, ALU.mult)
                link(v.scalar_tensor_tensor(wk[:, 0:1], pw[:, 0:1], 2.0 ** (-2 * TOP), pw[:, 1:2],
                                            ALU.mult, ALU.mult))
                v.tensor_copy(g_scale[:, which:which + 1], wk[:, 0:1])
                link(v.scalar_tensor_tensor(u_scale[:, which:which + 1], ip[:, 0:1],
                                            2.0 ** (-2 * TOP - 3), ip[:, 1:2], ALU.mult, ALU.mult))
                link(v.scalar_tensor_tensor(wk[:, 1:2], pw[:, 0:1], 2.0 ** (3 - TOP), pw[:, 3:4],
                                            ALU.mult, ALU.mult))
                link(v.tensor_tensor(wk[:, 2:3], pw[:, 0:1], pw[:, 2:3], ALU.mult))
                link(v.tensor_tensor(wk[:, 3:4], wk[:, 2:3], pw[:, 1:2], ALU.mult))
                link(v.tensor_tensor(y_scale[:, which:which + 1], wk[:, 1:2], wk[:, 3:4], ALU.mult))
                link(v.reciprocal(y_unit[:, which:which + 1], y_scale[:, which:which + 1]))
                v.tensor_copy(wk[:, 4:5], y_unit[:, which:which + 1]).then_inc(done, 1)

            dve.wait_ge(peaks_all_a, 1)
            scales(0, scale_a)

            def lo(dst, src, s, hi, done):
                v.scalar_tensor_tensor(dst, src, s, hi, ALU.mult, ALU.subtract).then_inc(done, 1)

            def x_lo(t):
                b = ds(t * TB, TB)
                dve.wait_ge(x1_hi, t + 1)
                lo(x1s[:, b, 1], x1t[:, ds(t * TILE, TILE)].rearrange("p (b s) -> p b s", s=S),
                   scale[:, 0, 0:1], x1s[:, b, 0], x1_lo)

            def w_lo(kind, e, which, done):
                lo(w16[:, kind, ds(e * WSTRIDE + F, F)],
                   w32[:, kind, ds(e, 1)].rearrange("p u f -> p (u f)"),
                   scale[:, which, kind + 1:kind + 2], w16[:, kind, ds(e * WSTRIDE, F)], done)

            dve.wait_ge(ws_hi, 1)
            w_lo(0, SHARED, 0, ws_lo)
            x_lo(0)
            dve.wait_ge(ws_hi, 2)
            w_lo(1, SHARED, 0, ws_lo)
            dve.wait_ge(ws_hi, 3)
            w_lo(2, SHARED, 0, ws_lo)

            def hidden(st, k, c, width, which):
                dve.wait_ge(st.gelu[c], k + 1)
                first = isinstance(k, int) and k == 0
                if c >= 2:
                    dve.wait_ge(st.hidden_hi[c - 2], k + 1)
                    dve.wait_ge(st.hidden_lo[c - 2], k + 1)
                elif not first:
                    dve.wait_ge(st.hidden_hi[CHUNKS + c - 2], k)
                    dve.wait_ge(st.hidden_lo[CHUNKS + c - 2], k)
                v.scalar_tensor_tensor(hid[:, c % 2, 0:width], ps_up[:, c % 2, 0:width],
                                       u_scale[:, which:which + 1], act_g[:, c % 2, 0:width],
                                       ALU.mult, ALU.mult).then_inc(st.hidden[c], 1)

            def hidden_lo(st, k, c, par, width):
                dve.wait_ge(st.hidden_hi[c], k + 1)
                v.tensor_tensor(hid_lo[:, par, c, 0:width], hid[:, c % 2, 0:width],
                                hid_hi[:, par, c, 0:width], ALU.subtract
                                ).then_inc(st.hidden_lo[c], 1)

            def stage_start(prev):
                for c in range(CHUNKS - 2, CHUNKS):
                    dve.wait_ge(prev.hidden_hi[c], prev.n)
                    dve.wait_ge(prev.hidden_lo[c], prev.n)

            def units(st, k, j, width, which, own_lo, between):
                par = (st.parity + j) % 2
                for c in range(CHUNKS):
                    hidden(st, k, c, width, which)
                    if c >= 1 and own_lo:
                        hidden_lo(st, k, c - 1, par, width)
                    if c == 2 and between is not None:
                        between()
                if own_lo:
                    hidden_lo(st, k, CHUNKS - 1, par, width)

            def take_base(k, par):
                dve.wait_ge(stage_a.down, k + 1)
                v.tensor_scalar(base[:, ds(k, 1)].rearrange("p u n -> p (u n)"), ps_down[:, par],
                                y_scale[:, 0:1], None, ALU.mult).then_inc(stage_a.taken, 1)

            units(stage_a, 0, 0, TILE, 0, False, lambda: x_lo(1))
            x_lo(2)
            dve.wait_ge(down_squares, 1)
            root = peak[:, 1, 3:4].bitcast(I32)
            link(v.tensor_scalar(root, tmp_c[:, 15:16].bitcast(I32), 1, None, ALU.arith_shift_right))
            v.tensor_scalar(root, root, float(127 << 22), None, ALU.add)
            dve.wait_ge(gate_in, 16)
            dve.wait_ge(up_in, 16)
            v.tensor_reduce(peak[:, 1, 2:3], w32[:, 1, 0:E].rearrange("p e f -> p (e f)"), AX.X,
                            ALU.max, apply_absolute_value=True)
            v.tensor_reduce(peak[:, 1, 1:2], w32[:, 0, 0:E].rearrange("p e f -> p (e f)"), AX.X,
                            ALU.max, apply_absolute_value=True)
            v.tensor_copy(peak[:, 1, 0:1], peak_all[:, 0, 0:1]).then_inc(peaks_b, 1)
            units(stage_a, 1, 1, TILE, 0, False, lambda: take_base(0, stage_a.parity))

            dve.wait_ge(maps_ready, 1)
            dve.wait_ge(rows_out, 1)
            link(v.tensor_scalar(row_c, row_z, 512.0, None, ALU.add))
            link(v.scalar_tensor_tensor(row_c, row_z, 0.0, row_c, ALU.is_lt, ALU.mult))
            link(v.scalar_tensor_tensor(row_a, row_z, 0.0, row_a, ALU.is_ge, ALU.mult))
            link(v.tensor_tensor(dst_i[:], row_c, row_a, ALU.add))
            link(v.tensor_scalar(src_i[:], dst_i[:], B - 1, None, ALU.bitwise_and))
            link(v.tensor_tensor(cmp_b, block_slot[:], ends[0:1, 0:E - 1].rearrange(
                "p (u e) -> p u e", u=1).broadcast_to([1, BLOCKS, E - 1]), ALU.is_ge))
            link(v.tensor_reduce(exp_f[:], cmp_b, AX.X, ALU.add))
            link(v.tensor_scalar(exp_i[:], exp_f[:], float(WSTRIDE), None, ALU.mult))
            dve.wait_ge(peaks_all_b, 1)
            scales(1, scale_b)
            link(v.tensor_tensor(
                w_slot.rearrange("p (n j) -> p n j", j=QB), w_slot.rearrange("p (n j) -> p n j", j=QB),
                quarter[:].rearrange("p (u j) -> p u j", u=1).broadcast_to([P, BLOCKS * GQ, QB]),
                ALU.mult))
            link(v.tensor_reduce(slot_w[:], w_slot.rearrange("p (n j) -> p n j", j=QB), AX.X, ALU.add))
            v.tensor_scalar(slot_w[:], slot_w[:], y_scale[:, 1:2], None, ALU.mult).then_inc(routed, 1)

            for k in range(2, FIRST):
                par = (stage_a.parity + k) % 2
                units(stage_a, k, k % 2, TILE, 0, False, lambda: take_base(k - 1, 1 - par))
                mine = share(3 * E, k - 2, FIRST - 2)
                dve.wait_ge(we_hi, mine.stop)
                for n in mine:
                    w_lo(n % 3, n // 3, 1, we_lo)

            def take_block(k, j, par):
                dve.wait_ge(stage_b.down, k + 1)
                dve.wait_ge(scattered[j], (k - j) * (8 * GROUP))
                v.tensor_tensor(y_sb[:, j], ps_down[:, par, 0:GW].rearrange(
                    "p (q c) -> p q c", q=GQ), slot_w[:, ds(k * GQ, GQ)].rearrange(
                        "p (q u) -> p q u", u=1).broadcast_to([P, GQ, C]), ALU.mult
                    ).then_inc(stage_b.taken, 1)

            stage_start(stage_a)

            def expert_block(k, j):
                par = (stage_b.parity + j) % 2
                if isinstance(k, int) and k == 0:
                    between = lambda: take_base(FIRST - 1, 1 - par)
                else:
                    between = lambda: take_block(k - 1, 1 - j, 1 - par)
                units(stage_b, k, j, GW, 1, True, between)
            steps(dve, BLOCKS, expert_block)

            def take_out(k, par):
                dve.wait_ge(stage_c.down, k + 1)
                dve.wait_ge(back_sum, k + 1)
                tile = ring[:, 2 * ((FIRST + k) % 2)].rearrange("p q c -> p (q c)")
                v.scalar_tensor_tensor(tile, ps_down[:, par], y_scale[:, 0:1], tile, ALU.mult,
                                       ALU.add).then_inc(stage_c.taken, 1)

            stage_start(stage_b)
            for k in range(LATER):
                par = (stage_c.parity + k) % 2
                if k == 0:
                    between = lambda: take_block(BLOCKS - 1, (BLOCKS - 1) % 2, 1 - par)
                else:
                    between = lambda: take_out(k - 1, 1 - par)
                units(stage_c, k, k % 2, TILE, 0, True, between)
            take_out(LATER - 1, stage_c.last_parity)

        @block.gpsimd
        def _(pool):
            g = nc.gpsimd
            chain = [0]

            def link(ins):
                chain[0] += 1
                ins.then_inc(pool_chain, 1)
                pool.wait_ge(pool_chain, chain[0])

            link(g.memset(ident[:], 0.0))
            g.affine_select(out=ident[:], in_=ident[:], compare_op=ALU.not_equal, fill=1.0, base=0,
                            pattern=[[-1, P]], channel_multiplier=1)
            link(g.memset(adapter_rows[:], 1.0))
            link(g.affine_select(out=adapter_rows[:], in_=adapter_rows[:], compare_op=ALU.is_ge,
                                 fill=0.0, base=0, pattern=[[1, P]], channel_multiplier=-R))
            g.affine_select(out=adapter_rows[:], in_=adapter_rows[:], compare_op=ALU.is_ge, fill=0.0,
                            base=R - 1, pattern=[[-1, P]], channel_multiplier=R).then_inc(consts, 1)
            iota = dict(allow_small_or_imprecise_dtypes=True, channel_multiplier=0)
            g.iota(rev[:], pattern=[[-1, E]], base=E, **iota)
            g.iota(fills[:], pattern=[[0, E], [GROUP, FILLS]], base=0, **iota)
            link(g.memset(upto[:], float(GROUP)))
            g.affine_select(out=upto[:], in_=upto[:], compare_op=ALU.is_ge, fill=0.0, base=0,
                            pattern=[[1, E], [-1, E]], channel_multiplier=0)
            g.memset(ones[:], 1.0).then_inc(consts, 1)
            link(g.memset(before_me[:], 1.0))
            g.affine_select(out=before_me[:], in_=before_me[:], compare_op=ALU.is_gt, fill=0.0, base=0,
                            pattern=[[1, P]], channel_multiplier=-1).then_inc(consts2, 1)
            g.memset(ones_h[:], 1.0)
            g.memset(b128_h[:], float(B))
            g.iota(batch_m512[:], pattern=[[0, 1]], base=-512, channel_multiplier=1,
                   allow_small_or_imprecise_dtypes=True)
            g.iota(slot_id, pattern=[[1, SLOTS]], base=0, **iota)
            g.iota(land_id, pattern=[[1, SLOTS]], base=LAND, **iota)
            g.iota(block_slot[:], pattern=[[GROUP, BLOCKS], [0, E - 1]], base=0, **iota)
            link(g.memset(quarter[:], 1.0))
            link(g.affine_select(out=quarter[:], in_=quarter[:], compare_op=ALU.is_ge, fill=0.0, base=0,
                                 pattern=[[-S, QB]], channel_multiplier=1))
            link(g.affine_select(out=quarter[:], in_=quarter[:], compare_op=ALU.is_ge, fill=0.0,
                                 base=S - 1, pattern=[[S, QB]], channel_multiplier=-1))

            pool.wait_ge(pos_ready, 1)
            g.tensor_scalar(slot1, slot_id, pos[:, 0:1], None, ALU.is_equal)
            g.tensor_scalar(slot2, slot_id, pos[:, 1:2], None, ALU.is_equal)
            g.tensor_scalar(below_h[:, 0], slot_id, pos[:, 0:1], None, ALU.is_gt)
            link(g.tensor_scalar(below_h[:, 1], slot_id, pos[:, 1:2], None, ALU.is_gt))
            g.tensor_tensor(taken_h[:], slot1, slot2, ALU.add)
            g.tensor_copy(second_h[:], slot2)
            g.tensor_tensor(below_h[:, 0], below_h[:, 0], below_h[:, 1], ALU.add).then_inc(maps_ready, 1)

            pool.wait_ge(peaks_a, NT + 2)
            g.partition_all_reduce(peak_all[:, 0], peak[:, 0], P, ABSMAX).then_inc(peaks_all_a, 1)

            pool.wait_ge(scale_a, 1)
            for k in range(FIRST):
                par = (stage_a.parity + k) % 2
                t = k + NT - FIRST
                for c in range(CHUNKS):
                    pool.wait_ge(stage_a.hidden_hi[c], k + 1)
                    g.tensor_tensor(hid_lo[:, par, c], hid[:, c % 2], hid_hi[:, par, c], ALU.subtract
                                    ).then_inc(stage_a.hidden_lo[c], 1)
                    if c == 0:
                        link(g.tensor_tensor(x_scaled, x1t[:, t * TILE:t * TILE + TILE],
                                             scale[:, 0, 0:1].broadcast_to([P, TILE]), ALU.mult))
                    if c == 1:
                        pool.wait_ge(x1_hi, t + 1)
                        pool.wait_ge(x1_lo, t)
                        b = slice(t * TB, t * TB + TB)
                        g.tensor_tensor(x1s[:, b, 1], x_scaled.rearrange("p (b s) -> p b s", s=S),
                                        x1s[:, b, 0], ALU.subtract).then_inc(x1_lo, 1)
                if k == 1:
                    pool.wait_ge(peaks_b, 1)
                    g.partition_all_reduce(peak_all[:, 1], peak[:, 1], P, ABSMAX
                                           ).then_inc(peaks_all_b, 1)

            pool.wait_ge(routed, 1)
            pool.wait_ge(x1_lo, NT)
            pool.wait_ge(x1_hi, NT)

            def gather(k, j):
                par = (stage_b.parity + j) % 2
                if not isinstance(k, int) or k >= 2:
                    pool.wait_ge(stage_b.gate_up[CHUNKS - 1], k - 1)
                for a in range(0, GROUP, QB):
                    src = values(ET.Pool, src_i[0:1, ds(k * GROUP + a, QB)], 0, B - 1)
                    for i in range(QB):
                        cp = g.tensor_copy(
                            gathered[:, par, a + i].rearrange("p h s -> p (h s)"),
                            x1s[:, ds(src[i], 1)].rearrange("p u h s -> p (u h s)"))
                cp.then_inc(slots_in, 1)
            steps(pool, BLOCKS, gather)

            def sums(t, j):
                pool.wait_ge(back_in[j], (t - j + 2) * 16)
                y0, y1 = (ring[:, 2 * j + h].rearrange("p q c -> p (q c)") for h in range(2))
                if t < FIRST:
                    link(g.tensor_tensor(y0, y0, y1, ALU.add))
                    g.tensor_tensor(base[:, t], base[:, t], y0, ALU.add).then_inc(base_sum, 1)
                else:
                    g.tensor_tensor(y0, y0, y1, ALU.add).then_inc(back_sum, 1)
            pool.wait_ge(stage_a.taken, FIRST)
            for t in range(NT):
                sums(t, t % 2)

    return nc


_INS = ["x", "cond_8", "L0_cond_W_base", "L0_cond_b_base", "L0_cond_As", "L0_cond_Bs",
        "L1_cond_skill_gate", "L1_cond_skill_up", "L1_cond_skill_down", "L1_cond_shared_gate",
        "L1_cond_shared_up", "L1_cond_shared_down"]
_OUT = ((128, 32, 128), "float32")


def kernel(**inputs):
    import numpy as _np
    import concourse.bacc as _bacc
    from concourse import mybir as _mybir
    from concourse.bass_utils import run_bass_kernel_spmd as _run

    nc = _bacc.Bacc("TRN2", target_bir_lowering=False, num_devices=1)
    arrays, args = {}, []
    for name in _INS:
        a = _np.ascontiguousarray(inputs[name])
        arrays[f"in_{name}"] = a
        args.append(nc.dram_tensor(f"in_{name}", a.shape, _mybir.dt.from_np(a.dtype),
                                   kind="ExternalInput").ap())
    out = nc.dram_tensor("out_0", _OUT[0], _mybir.dt.from_np(_np.dtype(_OUT[1])),
                         kind="ExternalOutput").ap()
    lora_moe_kernel(nc, *args, out)
    r = _run(nc, [arrays], core_ids=[0])
    return r.results[0]["out_0"]
```

```python
from contextlib import ExitStack

import concourse.bass as bass
from concourse import mybir

ALU = mybir.AluOpType
ACT = mybir.ActivationFunctionType
AX = mybir.AxisListType
ET = mybir.EngineType
F16 = mybir.dt.float16
F32 = mybir.dt.float32
I32 = mybir.dt.int32
ABSMAX = bass.bass_isa.ReduceOp.absmax
ds = bass.ds

P = 128
EXPONENT_MASK = 0x7F800000
TINY = 2.0 ** -24
TOP = 14
MASKED = -3.0e38


def ceil_div(a, b):
    return -(-a // b)


class Stage:

    def __init__(self, sem, name, n, chunks, parity):
        self.n, self.parity = n, parity
        self.last_parity = (parity + n - 1) % 2
        self.gate = [sem(f"{name}_gate_{c}") for c in range(chunks)]
        self.up = [sem(f"{name}_up_{c}") for c in range(chunks)]
        self.gelu = [sem(f"{name}_gelu_{c}") for c in range(chunks)]
        self.hidden = [sem(f"{name}_hidden_{c}") for c in range(chunks)]
        self.hidden_hi = [sem(f"{name}_hidden_hi_{c}") for c in range(chunks)]
        self.hidden_lo = [sem(f"{name}_hidden_lo_{c}") for c in range(chunks)]
        self.down = sem(f"{name}_down")
        self.taken = sem(f"{name}_taken")


def lora_moe_kernel(nc, x, cond, w_base, b_base, lora_a, lora_b, skill_gate, skill_up, skill_down,
                    shared_gate, shared_up, shared_down, out):
    B, S, C = x.shape
    E, R, _ = lora_a.shape
    F = shared_gate.shape[1]
    LORA_SCALING = 32.0 / R
    MOE_SCALE = 1.0 / 12
    assert B == P and C == P and E * R == P and E == 8 and P % S == 0

    TILE = 512
    TB = TILE // S
    NT = B * S // TILE
    SUB = TILE // P
    QB = P // S
    CHUNKS = F // P
    XRING = 4
    FIRST = 5
    LATER = NT - FIRST
    GROUP = 12
    GW = GROUP * S
    GQ = GW // P
    BLOCKS = (2 * B + E * (GROUP - 1)) // GROUP
    SLOTS = BLOCKS * GROUP
    FILLS = ceil_div(B, GROUP)
    LAND = 2 * B
    WSTRIDE = 2 * F
    SP_SLOTS = GROUP - QB
    LAG = 3
    SHARED = E
    FINALS = list(range(FIRST, NT)) + list(range(FIRST))
    STORES = [FIRST] + list(range(FIRST)) + list(range(FIRST + 1, NT))
    assert FIRST % 2 == 1 and LATER % 2 == 1 and NT % XRING == 0 and GW % P == 0

    with ExitStack() as ctx:
        def sb(name, shape, dt):
            return ctx.enter_context(nc.sbuf_tensor(name, shape, dt))

        def psum(name, shape):
            return ctx.enter_context(nc.psum_tensor(name, shape, F32))

        def sem(name):
            return ctx.enter_context(nc.semaphore(name))

        expert_out = nc.dram_tensor("expert_out", [SLOTS, S, C], F32, kind="Internal").ap()

        ps_gate = psum("ps_gate", [P, 2, TILE])
        ps_up = psum("ps_up", [P, 2, TILE])
        ps_down = psum("ps_down", [P, 2, TILE])
        ps_misc = psum("ps_misc", [P, 2, TILE])
        ps_xt, ps_lora, ps_x1 = ps_gate, ps_up, ps_down

        ident = sb("ident", [P, P], F32)
        adapter_rows = sb("adapter_rows", [E, P], F32)
        before_me = sb("before_me", [P, P], F32)
        ones = sb("ones", [P, P], F32)
        ones_h = sb("ones_h", [P, 1], F16)
        batch_m512 = sb("batch_m512", [P, 1], F16)
        b128_h = sb("b128_h", [P, 1], F16)
        rev = sb("rev", [P, E], F32)
        fills = sb("fills", [P, E, FILLS], F32)
        upto = sb("upto", [P, E, E], F32)
        quarter = sb("quarter", [P, QB], F32)
        block_slot = sb("block_slot", [1, BLOCKS, E - 1], F32)

        cond_sb = sb("cond_sb", [P, E], F32)
        bias = sb("bias", [P, 1], F32)
        small_t = sb("small_t", [P, 3, P], F32)
        cond_t = sb("cond_t", [E, P], F32)
        lora_w = sb("lora_w", [P, B], F32)
        ring = sb("ring", [P, XRING, SUB, C], F32)
        pair = sb("pair", [P, 2, TILE], F32)
        x1t = sb("x1t", [P, B * S], F32)
        x1s = sb("x1s", [P, B, 2, S], F16)
        w32 = sb("w32", [P, 3, E + 1, F], F32)
        w16 = sb("w16", [P, 3, (E + 1) * WSTRIDE], F16)
        base = sb("base", [P, FIRST, TILE], F32)

        gate_e = sb("gate_e", [P, E], F32)
        choice = sb("choice", [P, 2, E], F32)
        tmp_e = sb("tmp_e", [P, 4, E], F32)
        tmp_c = sb("tmp_c", [P, 16], F32)
        chosen = sb("chosen", [P, E], F32)
        tmp_fill = sb("tmp_fill", [P, E, FILLS], F32)
        tmp_ee = sb("tmp_ee", [P, E, E], F32)
        n_blocks = sb("n_blocks", [P, E], F32)
        ends = sb("ends", [P, E], F32)
        place = sb("place", [P, E], F32)
        pos = sb("pos", [P, 2], F32)
        w_col = sb("w_col", [P, 2, P], F32)
        taken_h = sb("taken_h", [P, SLOTS], F16)
        second_h = sb("second_h", [P, SLOTS], F16)
        below_h = sb("below_h", [P, 2, SLOTS], F16)
        dst_i = sb("dst_i", [1, SLOTS], I32)
        src_i = sb("src_i", [1, SLOTS], I32)
        exp_f = sb("exp_f", [1, BLOCKS], F32)
        exp_i = sb("exp_i", [1, BLOCKS], I32)
        dst_token = sb("dst_token", [P, BLOCKS], I32)
        dst_now = sb("dst_now", [P, 2], I32)
        token_i = sb("token_i", [P, 1], I32)
        slot_w = sb("slot_w", [P, BLOCKS * GQ], F32)

        peak = sb("peak", [P, 2, 4], F32)
        peak_all = sb("peak_all", [P, 2, 4], F32)
        tile_peak = sb("tile_peak", [P, NT], F32)
        p2 = sb("p2", [P, 2, 4], F32)
        ip2 = sb("ip2", [P, 2, 4], F32)
        scale = sb("scale", [P, 2, 4], F32)
        work = sb("work", [P, 2, 6], F32)
        g_scale = sb("g_scale", [P, 2], F32)
        u_scale = sb("u_scale", [P, 2], F32)
        y_scale = sb("y_scale", [P, 2], F32)
        y_unit = sb("y_unit", [P, 2], F32)

        act_g = sb("act_g", [P, 2, TILE], F32)
        hid = sb("hid", [P, 2, TILE], F32)
        hid_hi = sb("hid_hi", [P, 2, CHUNKS, TILE], F16)
        hid_lo = sb("hid_lo", [P, 2, CHUNKS, TILE], F16)
        gathered = sb("gathered", [P, 2, GROUP, 2, S], F16)
        y_sb = sb("y_sb", [P, 2, GQ, C], F32)

        slot1 = hid[:, 0, 0:SLOTS]
        slot2 = hid[:, 1, 0:SLOTS]
        back = w32[:].rearrange("p a e f -> p (a e f)")[:, 0:NT * 2 * TILE].rearrange(
            "p (t h n) -> p t h n", h=2, n=TILE)
        x_scaled = y_sb[:].rearrange("p j q c -> p (j q c)")[:, 0:TILE]
        wb_sb, la_sb, lb_sb = (base[:, 2, i * P:i * P + P] for i in range(3))
        xt, mixed = pair, base[:, 0:2]
        x1_unit = pair
        slot_id = act_g[:, 0, 0:SLOTS]
        land_id = act_g[0:1, 1, 0:SLOTS]
        spare = ring[:].rearrange("p t q c -> p (t q c)")
        row_z, row_a, row_c = (spare[0:1, i * SLOTS:(i + 1) * SLOTS] for i in range(3))
        w_slot = spare[:, 3 * SLOTS:4 * SLOTS]
        tmp_cols = spare[:, 5 * SLOTS:5 * SLOTS + BLOCKS * QB]
        tmp_cols2 = spare[:, 5 * SLOTS + BLOCKS * QB:5 * SLOTS + BLOCKS * (QB + 1)]
        cmp_b = spare[0:1, 4 * SLOTS:4 * SLOTS + BLOCKS * (E - 1)].rearrange(
            "p (k e) -> p k e", e=E - 1)

        cond_in, small_in = sem("cond_in"), sem("small_in")
        x_in = [sem(f"x_in_{i}") for i in range(XRING)]
        shared_in = sem("shared_in")
        gate_in, up_in, down_in = sem("gate_in"), sem("up_in"), sem("down_in")
        consts, consts2 = sem("consts"), sem("consts2")
        pool_chain, dve_chain, act_chain = sem("pool_chain"), sem("dve_chain"), sem("act_chain")
        small_tr, small_out, lora_w_ps, lora_w_ready = (
            sem("small_tr"), sem("small_out"), sem("lora_w_ps"), sem("lora_w_ready"))
        neg_max, exped, chosen_ready, ranks, pos_ready, w_col_ready = (
            sem("neg_max"), sem("exped"), sem("chosen_ready"), sem("ranks"), sem("pos_ready"),
            sem("w_col_ready"))
        maps_ready, rows_ps, rows_out, routed = (
            sem("maps_ready"), sem("rows_ps"), sem("rows_out"), sem("routed"))
        dst_row, dst_all, offsets_set = sem("dst_row"), sem("dst_all"), sem("offsets_set")
        xt_ps, xt_out, lora_ps, lora_mixed, x1_ps, x1_out = (
            sem("xt_ps"), sem("xt_out"), sem("lora_ps"), sem("lora_mixed"), sem("x1_ps"),
            sem("x1_out"))
        peaks_a, peaks_b, peaks_all_a, peaks_all_b, scale_a, scale_b = (
            sem("peaks_a"), sem("peaks_b"), sem("peaks_all_a"), sem("peaks_all_b"),
            sem("scale_a"), sem("scale_b"))
        down_squares = sem("down_squares")
        x1_hi, x1_lo = sem("x1_hi"), sem("x1_lo")
        ws_hi, ws_lo, we_hi, we_lo = sem("ws_hi"), sem("ws_lo"), sem("we_hi"), sem("we_lo")
        x1_unit_a, x1_unit_c = sem("x1_unit_a"), sem("x1_unit_c")
        slots_in, scattered = sem("slots_in"), [sem("scattered_0"), sem("scattered_1")]
        group_scattered = [sem("group_scattered_0"), sem("group_scattered_1")]
        back_in = [sem(f"back_in_{t}") for t in range(NT)]
        back_sum, finished, stored = sem("back_sum"), sem("finished"), sem("stored")
        stage_a = Stage(sem, "first", FIRST, CHUNKS, 0)
        stage_b = Stage(sem, "block", BLOCKS, CHUNKS, (stage_a.last_parity + 1) % 2)
        stage_c = Stage(sem, "later", LATER, CHUNKS, (stage_b.last_parity + 1) % 2)

        x_dram = x.rearrange("b s c -> (b s) c").rearrange("(t q p) c -> t p q c", q=SUB, p=P)
        out_dram = out.rearrange("b s c -> (b s) c").rearrange("(t q p) c -> t p q c", q=SUB, p=P)
        rows_dram = expert_out[0:2 * B].rearrange("r s c -> (r s) c").rearrange(
            "(t q p) c -> t p q c", q=SUB, p=P)

        def values(engine, ap, least, most):
            _, v = nc.values_load_multi_w_load_instructions(
                ap, engines=[engine], min_val=least, max_val=most,
                skip_runtime_bounds_check_because="the routing gives values in these bounds")
            return v

        def steps(e, n, step, peel=2):
            for k in range(peel):
                step(k, k % 2)
            turns = (n - peel) // 2
            with e.Fori(peel, peel + 2 * turns - 1, 2) as k:
                step(k, 0)
                step(k + 1, 1)
            if n % 2:
                step(n - 1, 0)

        def share(n, i, of):
            return range(n * i // of, n * (i + 1) // of)

        block = ctx.enter_context(nc.Block())

        @block.sync
        def _(sp):
            sp.dma_start(cond_sb[:], cond).then_inc(cond_in, 16)
            sp.dma_start(wb_sb, w_base).then_inc(small_in, 16)
            sp.dma_start(la_sb, lora_a.rearrange("e r c -> (e r) c")).then_inc(small_in, 16)
            sp.dma_start(lb_sb.rearrange("o (e r) -> o e r", e=E), lora_b.rearrange("e o r -> o e r")).then_inc(small_in, 16)
            sp.dma_start(bias[:], b_base.rearrange("(o u) -> o u", u=1)).then_inc(small_in, 16)
            for r in range(XRING):
                sp.dma_start(ring[:, r], x_dram[r]).then_inc(x_in[r], 16)
            with sp.Fori(XRING, NT - XRING + 1, XRING) as t:
                for r in range(XRING):
                    sp.wait_ge(xt_ps, t - XRING + r + 1)
                    sp.dma_start(ring[:, r], x_dram[ds(t + r, 1)].rearrange("u p q c -> p (u q) c")
                                 ).then_inc(x_in[r], 16)

            sp.wait_ge(routed, 1)

            def scatter(k, j):
                rows = values(ET.SP, dst_i[0:1, ds(k * GROUP, SP_SLOTS)], 0, SLOTS - 1)
                sp.wait_ge(stage_b.taken, k + 1)
                for i in range(SP_SLOTS):
                    part = i % QB * S
                    sp.dma_start(expert_out[ds(rows[i], 1)].rearrange("u s c -> (u s) c"),
                                 y_sb[part:part + S, j, i // QB]).then_inc(scattered[j], 16)
            steps(sp, BLOCKS, scatter)

            for j in range(2):
                sp.wait_ge(scattered[j], 16 * SP_SLOTS * BLOCKS // 2)
                sp.wait_ge(group_scattered[j], 16 * BLOCKS // 2)
            for t in FINALS:
                for h in range(2):
                    sp.dma_start(back[:, t, h].rearrange("p (q c) -> p q c", q=SUB),
                                 rows_dram[h * NT + t]).then_inc(back_in[t], 16)
            for n, t in enumerate(STORES):
                sp.wait_ge(finished, n + 1)
                done = base[:, t] if t < FIRST else back[:, t, 0]
                sp.dma_start(out_dram[t], done.rearrange("p (q c) -> p q c", q=SUB)
                             ).then_inc(stored, 16)
            sp.wait_ge(stored, 16 * NT)

        @block.tensor
        def _(pe):
            pe.wait_ge(consts, 1)
            pe.wait_ge(small_in, 64)
            pe.wait_ge(cond_in, 16)
            pe.transpose(ps_misc[:, 0, 0:P], wb_sb, ident[:])
            pe.transpose(ps_misc[:, 0, P:2 * P], la_sb, ident[:])
            pe.transpose(ps_misc[:, 0, 2 * P:3 * P], lb_sb, ident[:])
            pe.transpose(ps_misc[0:E, 0, 3 * P:4 * P], cond_sb[:], ident[:]).then_inc(small_tr, 1)
            pe.wait_ge(small_out, 1)
            pe.matmul(ps_misc[:, 1, 0:B], adapter_rows[:], cond_t[:], start=True, stop=True
                      ).then_inc(lora_w_ps, 1)
            pe.wait_ge(chosen_ready, 1)
            pe.wait_ge(consts2, 1)
            pe.wait_ge(lora_w_ready, 1)
            pe.matmul(ps_misc[:, 1, 0:E], before_me[:], chosen[:], start=True, stop=True)
            pe.matmul(ps_misc[:, 1, E:2 * E], ones[:], chosen[:], start=True, stop=True
                      ).then_inc(ranks, 1)

            def turn(t, r, in_flight):
                pe.wait_ge(x_in[r], in_flight)
                if not isinstance(t, int) or t >= 2:
                    pe.wait_ge(xt_out, t - 1)
                for q in range(SUB):
                    mm = pe.transpose(ps_xt[:, r % 2, q * P:q * P + P], ring[:, r, q], ident[:])
                mm.then_inc(xt_ps, 1)

            def products(t, r):
                pe.wait_ge(xt_out, t + 1)
                if not isinstance(t, int) or t >= 2:
                    pe.wait_ge(x1_out, t - 1)
                pe.matmul(ps_lora[:, r % 2], small_t[:, 1], xt[:, r % 2], start=True, stop=True
                          ).then_inc(lora_ps, 1)
                pe.matmul(ps_x1[:, r % 2], small_t[:, 0], xt[:, r % 2], start=True, stop=False)

            def adapters(t, r):
                pe.wait_ge(lora_mixed, t + 1)
                pe.matmul(ps_x1[:, r % 2], small_t[:, 2], mixed[:, r % 2], start=False, stop=True
                          ).then_inc(x1_ps, 1)

            turn(0, 0, 16)
            for t in range(XRING - 1):
                products(t, t)
                turn(t + 1, t + 1, 16)
                adapters(t, t)
            with pe.Fori(XRING, NT - XRING + 1, XRING) as t:
                for r in range(XRING):
                    products(t + (r - 1), (r - 1) % XRING)
                    turn(t + r, r, 4 * (t + XRING))
                    adapters(t + (r - 1), (r - 1) % XRING)
            products(NT - 1, XRING - 1)
            adapters(NT - 1, XRING - 1)

            pe.wait_ge(maps_ready, 1)
            pe.wait_ge(pos_ready, 1)
            pe.wait_ge(w_col_ready, 1)
            pe.matmul(ps_misc[0:1, 0, 0:SLOTS], batch_m512[:], taken_h[:], start=True, stop=False)
            pe.matmul(ps_misc[0:1, 0, 0:SLOTS], b128_h[:], second_h[:], start=False, stop=True)
            pe.matmul(ps_misc[0:1, 1, 0:SLOTS], ones_h[:], below_h[:, 0], start=True, stop=True)
            pe.wait_ge(x1_out, NT)
            pe.matmul(ps_down[:, 1, 0:SLOTS], w_col[:, 0], slot1, start=True, stop=False)
            pe.matmul(ps_down[:, 1, 0:SLOTS], w_col[:, 1], slot2, start=False, stop=True
                      ).then_inc(rows_ps, 1)

            def gate_up(st, prev, k, c, weights, moving):
                x_hi, x_lo, width = moving
                for kind, bank, reads, last, done in (
                        (0, ps_gate, st.gelu, prev and prev.gelu, st.gate),
                        (1, ps_up, st.hidden, prev and prev.hidden, st.up)):
                    if c >= 2:
                        pe.wait_ge(reads[c - 2], k + 1)
                    elif not isinstance(k, int) or k > 0:
                        pe.wait_ge(reads[CHUNKS + c - 2], k)
                    elif prev is not None:
                        pe.wait_ge(last[CHUNKS + c - 2], prev.n)
                    w_hi, w_lo = weights(kind, c * P), weights(kind, F + c * P)
                    o = bank[:, c % 2, 0:width]
                    pe.matmul(o, w_hi, x_hi, start=True, stop=False)
                    pe.matmul(o, w_hi, x_lo, start=False, stop=False)
                    pe.matmul(o, w_lo, x_hi, start=False, stop=True).then_inc(done[c], 1)

            def down(st, k, par, c, weights, subs):
                pe.wait_ge(st.hidden_hi[c], k + 1)
                pe.wait_ge(st.hidden_lo[c], k + 1)
                w_hi = weights(2, c * P)
                for q in range(subs):
                    o = ps_down[:, par, q * P:q * P + P]
                    pe.matmul(o, hid_hi[:, par, c, q * P:q * P + P], w_hi,
                              start=(c == 0 and q == 0), stop=False, skip_group_check=True)
                    pe.matmul(o, hid_lo[:, par, c, q * P:q * P + P], w_hi,
                              start=False, stop=False, skip_group_check=True)
                w_lo = weights(2, F + c * P)
                last = c == CHUNKS - 1
                for q in range(subs):
                    mm = pe.matmul(ps_down[:, par, q * P:q * P + P],
                                   hid_hi[:, par, c, q * P:q * P + P], w_lo, start=False,
                                   stop=last and st is stage_b, skip_group_check=True)
                if last and st is stage_b:
                    mm.then_inc(st.down, 1)

            def shared_weights(kind, at):
                a = SHARED * WSTRIDE + at
                return w16[:, kind, a:a + P]

            def expert_weights(offset):
                return lambda kind, at: w16[:, kind, at:][:, ds(offset, P)]

            def tile_moving(t):
                xs = x1s[:, t * TB:t * TB + TB]
                return xs[:, :, 0], xs[:, :, 1], TILE

            def block_moving(par):
                return gathered[:, par, :, 0], gathered[:, par, :, 1], GW

            def shared_down(st, k, par, c, x1_ready):
                down(st, k, par, c, shared_weights, SUB)
                if c == CHUNKS - 1:
                    pe.wait_ge(x1_ready, k + 1)
                    for q in range(SUB):
                        mm = pe.matmul(ps_down[:, par, q * P:q * P + P],
                                       x1_unit[:, par, q * P:q * P + P], ident[:],
                                       start=False, stop=True, skip_group_check=True)
                    mm.then_inc(st.down, 1)

            pe.wait_ge(ws_hi, 3)
            pe.wait_ge(ws_lo, 3)

            for k in range(FIRST):
                par = (stage_a.parity + k) % 2
                pe.wait_ge(x1_hi, k + 1)
                pe.wait_ge(x1_lo, k + 1)
                for c in range(CHUNKS):
                    gate_up(stage_a, None, k, c, shared_weights, tile_moving(k))
                    if k == 1 and c == 0:
                        pe.wait_ge(rows_out, 1)
                        pe.wait_ge(dst_row, 1)
                        pe.matmul(ps_misc[:, 0, 0:SLOTS], ones[0:1, :], row_c, start=True, stop=True
                                  ).then_inc(dst_all, 1)
                    if k > 0:
                        shared_down(stage_a, k - 1, 1 - par, c, x1_unit_a)

            pe.wait_ge(we_hi, 3 * E)
            pe.wait_ge(we_lo, 3 * E)
            pe.wait_ge(routed, 1)

            def expert_block(k, j):
                par = (stage_b.parity + j) % 2
                first = isinstance(k, int) and k == 0
                if first:
                    now = values(ET.PE, exp_i[0:1, 0:1], 0, (E - 1) * WSTRIDE)[0]
                else:
                    last, now = values(ET.PE, exp_i[0:1, ds(k - 1, 2)], 0, (E - 1) * WSTRIDE)
                pe.wait_ge(slots_in, k + 1)
                for c in range(CHUNKS):
                    gate_up(stage_b, stage_a, k, c, expert_weights(now), block_moving(par))
                    if first:
                        shared_down(stage_a, FIRST - 1, 1 - par, c, x1_unit_a)
                    else:
                        down(stage_b, k - 1, 1 - par, c, expert_weights(last), GQ)
            steps(pe, BLOCKS, expert_block)

            last = values(ET.PE, exp_i[0:1, BLOCKS - 1:BLOCKS], 0, (E - 1) * WSTRIDE)[0]
            for k in range(LATER):
                par = (stage_c.parity + k) % 2
                for c in range(CHUNKS):
                    gate_up(stage_c, stage_b, k, c, shared_weights, tile_moving(k + FIRST))
                    if k > 0:
                        shared_down(stage_c, k - 1, 1 - par, c, x1_unit_c)
                    elif c < 2:
                        for d in (2 * c, 2 * c + 1):
                            down(stage_b, BLOCKS - 1, 1 - par, d, expert_weights(last), GQ)
            pe.wait_ge(finished, 1)
            for c in range(CHUNKS):
                shared_down(stage_c, LATER - 1, stage_c.last_parity, c, x1_unit_c)

        @block.scalar
        def _(act):
            act.dma_start(w32[:, 0, SHARED], shared_gate).then_inc(shared_in, 16)
            act.dma_start(w32[:, 1, SHARED], shared_up).then_inc(shared_in, 16)
            act.dma_start(w32[:, 2, SHARED].rearrange("p (c h) -> p c h", c=CHUNKS),
                          shared_down.rearrange("(c p) h -> p c h", p=P)).then_inc(shared_in, 16)
            act.dma_start(w32[:, 2, 0:E].rearrange("p e (c h) -> p (e c) h", c=CHUNKS),
                          skill_down.rearrange("e (c p) h -> p (e c) h", p=P)).then_inc(down_in, 16)
            act.dma_start(w32[:, 0, 0:E], skill_gate.rearrange("e h i -> h e i")).then_inc(gate_in, 16)
            act.dma_start(w32[:, 1, 0:E], skill_up.rearrange("e h i -> h e i")).then_inc(up_in, 16)
            act.wait_ge(neg_max, 1)
            nc.scalar.activation(gate_e[:], cond_sb[:], ACT.Exp, bias=tmp_c[:, 1:2]).then_inc(exped, 1)
            act.wait_ge(small_tr, 1)
            nc.scalar.activation(small_t[:].rearrange("p a b -> p (a b)"), ps_misc[:, 0, 0:3 * P], ACT.Copy)
            nc.scalar.activation(cond_t[:], ps_misc[0:E, 0, 3 * P:4 * P], ACT.Copy).then_inc(small_out, 1)

            def copy_xt(t, j):
                act.wait_ge(xt_ps, t + 1)
                if not isinstance(t, int) or t >= 2:
                    act.wait_ge(x1_out, t - 1)
                nc.scalar.activation(xt[:, j], ps_xt[:, j], ACT.Copy).then_inc(xt_out, 1)
            steps(act, NT, copy_xt)
            act.wait_ge(down_in, 16)
            nc.scalar.activation(w16[:, 2, 0:E * F], w32[:, 2, 0:E].rearrange("p e f -> p (e f)"),
                                 ACT.Square, accum_out=tmp_c[:, 15:16]).then_inc(down_squares, 1)

            def split_hi(dst, src, s, done):
                nc.scalar.activation(dst, src, ACT.Copy, scale=s).then_inc(done, 1)

            def x_hi(t):
                split_hi(x1s[:, ds(t * TB, TB), 0], x1t[:, ds(t * TILE, TILE)].rearrange(
                    "p (b s) -> p b s", s=S), scale[:, 0, 0:1], x1_hi)

            def w_hi(kind, e, which, done):
                split_hi(w16[:, kind, ds(e * WSTRIDE, F)], w32[:, kind, ds(e, 1)].rearrange(
                    "p u f -> p (u f)"), scale[:, which, kind + 1:kind + 2], done)

            act.wait_ge(scale_a, 1)
            w_hi(0, SHARED, 0, ws_hi)
            x_hi(0)
            w_hi(1, SHARED, 0, ws_hi)
            w_hi(2, SHARED, 0, ws_hi)

            def gelu(st, prev, k, c, width, which):
                act.wait_ge(st.gate[c], k + 1)
                first = isinstance(k, int) and k == 0
                if c >= 2:
                    act.wait_ge(st.hidden[c - 2], k + 1)
                elif not first:
                    act.wait_ge(st.hidden[CHUNKS + c - 2], k)
                elif prev is not None:
                    act.wait_ge(prev.hidden[CHUNKS + c - 2], prev.n)
                nc.scalar.activation(act_g[:, c % 2, 0:width], ps_gate[:, c % 2, 0:width],
                                     ACT.Gelu_apprx_tanh, scale=g_scale[:, which:which + 1]
                                     ).then_inc(st.gelu[c], 1)

            def hidden_hi(st, prev, k, c, par, width):
                act.wait_ge(st.hidden[c], k + 1)
                if c == 0:
                    if not isinstance(k, int) or k >= 2:
                        act.wait_ge(st.down, k - 1)
                    elif k == 0 and prev is not None:
                        act.wait_ge(prev.down, prev.n - 1)
                nc.scalar.activation(hid_hi[:, par, c, 0:width], hid[:, c % 2, 0:width], ACT.Copy
                                     ).then_inc(st.hidden_hi[c], 1)

            def x1_in_units(st, k, par, t, done):
                if k >= 2:
                    act.wait_ge(st.down, k - 1)
                nc.scalar.activation(x1_unit[:, par], x1t[:, t * TILE:t * TILE + TILE], ACT.Copy,
                                     scale=y_unit[:, 0:1]).then_inc(done, 1)

            UNITS = FIRST * CHUNKS
            for k in range(FIRST):
                par = (stage_a.parity + k) % 2
                for c in range(CHUNKS):
                    n = k * CHUNKS + c
                    gelu(stage_a, None, k, c, TILE, 0)
                    if c >= 1:
                        hidden_hi(stage_a, None, k, c - 1, par, TILE)
                    if n % 2 == 0 and n // 2 + 1 < NT:
                        x_hi(n // 2 + 1)
                    if n == 4:
                        act.wait_ge(scale_b, 1)
                        act.wait_ge(down_squares, 1)
                    if n >= 4:
                        for i in share(3 * E, n - 4, UNITS - 4):
                            w_hi(i % 3, i // 3, 1, we_hi)
                hidden_hi(stage_a, None, k, CHUNKS - 1, par, TILE)

            def expert_block(k, j):
                par = (stage_b.parity + j) % 2
                for c in range(CHUNKS):
                    gelu(stage_b, stage_a, k, c, GW, 1)
                    if c >= 1:
                        hidden_hi(stage_b, stage_a, k, c - 1, par, GW)
                hidden_hi(stage_b, stage_a, k, CHUNKS - 1, par, GW)
            steps(act, BLOCKS, expert_block, 4)

            for k in range(LATER):
                par = (stage_c.parity + k) % 2
                x1_in_units(stage_c, k, par, k + FIRST, x1_unit_c)
                for c in range(CHUNKS):
                    gelu(stage_c, stage_b, k, c, TILE, 0)
                    if c >= 1:
                        hidden_hi(stage_c, stage_b, k, c - 1, par, TILE)
                hidden_hi(stage_c, stage_b, k, CHUNKS - 1, par, TILE)

        @block.vector
        def _(dve):
            v = nc.vector
            chain = [0]

            def link(ins):
                chain[0] += 1
                ins.then_inc(dve_chain, 1)
                dve.wait_ge(dve_chain, chain[0])

            dve.wait_ge(cond_in, 16)
            link(v.tensor_reduce(tmp_c[:, 0:1], cond_sb[:], AX.X, ALU.max))
            v.tensor_scalar(tmp_c[:, 1:2], tmp_c[:, 0:1], -1.0, None, ALU.mult).then_inc(neg_max, 1)
            dve.wait_ge(consts, 2)
            link(v.scalar_tensor_tensor(tmp_e[:, 0], cond_sb[:], tmp_c[:, 0:1], rev[:], ALU.is_equal,
                                        ALU.mult))
            link(v.tensor_reduce(tmp_c[:, 2:3], tmp_e[:, 0], AX.X, ALU.max))
            link(v.tensor_scalar(choice[:, 0], rev[:], tmp_c[:, 2:3], None, ALU.is_equal))
            link(v.scalar_tensor_tensor(tmp_e[:, 1], choice[:, 0], MASKED, cond_sb[:], ALU.mult,
                                        ALU.add))
            link(v.tensor_reduce(tmp_c[:, 3:4], tmp_e[:, 1], AX.X, ALU.max))
            link(v.scalar_tensor_tensor(tmp_e[:, 0], tmp_e[:, 1], tmp_c[:, 3:4], rev[:],
                                        ALU.is_equal, ALU.mult))
            link(v.tensor_reduce(tmp_c[:, 4:5], tmp_e[:, 0], AX.X, ALU.max))
            link(v.tensor_scalar(choice[:, 1], rev[:], tmp_c[:, 4:5], None, ALU.is_equal))
            v.tensor_tensor(chosen[:], choice[:, 0], choice[:, 1], ALU.add).then_inc(chosen_ready, 1)
            dve.wait_ge(exped, 1)
            link(v.tensor_reduce(tmp_c[:, 5:6], gate_e[:], AX.X, ALU.add))
            link(v.reciprocal(tmp_c[:, 6:7], tmp_c[:, 5:6]))
            link(v.tensor_scalar(tmp_e[:, 2], gate_e[:], tmp_c[:, 6:7], None, ALU.mult))
            link(v.tensor_tensor(tmp_e[:, 0:2], choice[:], tmp_e[:, 2:3].broadcast_to([P, 2, E]), ALU.mult))
            link(v.tensor_reduce(tmp_c[:, 7:9], tmp_e[:, 0:2], AX.X, ALU.add))
            link(v.tensor_reduce(tmp_c[:, 9:10], tmp_c[:, 7:9], AX.X, ALU.add))
            link(v.reciprocal(tmp_c[:, 10:11], tmp_c[:, 9:10]))
            link(v.tensor_scalar(tmp_c[:, 11:13], tmp_c[:, 7:9], tmp_c[:, 10:11], None, ALU.mult))
            link(v.tensor_scalar(tmp_c[:, 13:15], tmp_c[:, 11:13], MOE_SCALE, None, ALU.mult))
            link(v.scalar_tensor_tensor(tmp_c[:, 7:9], tmp_c[:, 11:13], 1.0 - MOE_SCALE,
                                        tmp_c[:, 13:15], ALU.mult, ALU.add))
            v.tensor_scalar(w_col[:, 0], ones[:], tmp_c[:, 7:8], None, ALU.mult)
            v.tensor_scalar(w_col[:, 1], ones[:], tmp_c[:, 8:9], None, ALU.mult).then_inc(w_col_ready, 1)
            dve.wait_ge(lora_w_ps, 1)
            v.tensor_scalar(lora_w[:], ps_misc[:, 1, 0:B], LORA_SCALING, None, ALU.mult
                            ).then_inc(lora_w_ready, 1)
            dve.wait_ge(ranks, 1)
            link(v.tensor_copy(tmp_e[:, 0:2].rearrange("p a e -> p (a e)"), ps_misc[:, 1, 0:2 * E]))
            link(v.tensor_tensor(tmp_fill[:], tmp_e[:, 1].rearrange("p (e u) -> p e u", u=1)
                                 .broadcast_to([P, E, FILLS]), fills[:], ALU.is_gt))
            link(v.tensor_reduce(n_blocks[:], tmp_fill[:], AX.X, ALU.add))
            link(v.tensor_tensor(tmp_ee[:], n_blocks[:].rearrange("p (u e) -> p u e", u=1)
                                 .broadcast_to([P, E, E]), upto[:], ALU.mult))
            link(v.tensor_reduce(ends[:], tmp_ee[:], AX.X, ALU.add))
            link(v.scalar_tensor_tensor(tmp_e[:, 2], n_blocks[:], -float(GROUP), ends[:], ALU.mult,
                                        ALU.add))
            link(v.tensor_tensor(place[:], tmp_e[:, 0], tmp_e[:, 2], ALU.add))
            link(v.tensor_tensor(tmp_e[:, 0:2], choice[:], place[:].rearrange("p (u e) -> p u e", u=1)
                                 .broadcast_to([P, 2, E]), ALU.mult))
            v.tensor_reduce(pos[:], tmp_e[:, 0:2], AX.X, ALU.add).then_inc(pos_ready, 1)

            dve.wait_ge(lora_w_ready, 1)

            def layer0(t, j):
                tok = ds(t * TILE, TILE)
                dve.wait_ge(lora_ps, t + 1)
                if not isinstance(t, int) or t >= 2:
                    dve.wait_ge(x1_ps, t - 1)
                v.tensor_tensor(mixed[:, j].rearrange("p (b s) -> p b s", s=S),
                                ps_lora[:, j].rearrange("p (b s) -> p b s", s=S),
                                lora_w[:, ds(t * TB, TB)].rearrange("p (b u) -> p b u", u=1)
                                .broadcast_to([P, TB, S]), ALU.mult).then_inc(lora_mixed, 1)
                dve.wait_ge(x1_ps, t + 1)
                v.scalar_tensor_tensor(x1t[:, tok], ps_x1[:, j], bias[:, 0:1], xt[:, j], ALU.add,
                                       ALU.add).then_inc(x1_out, 1)
                dve.wait_ge(x1_out, t + 1)
                v.tensor_reduce(tile_peak[:, ds(t, 1)], x1t[:, tok], AX.X, ALU.max,
                                apply_absolute_value=True).then_inc(peaks_a, 1)
            dve.wait_ge(small_in, 64)
            steps(dve, NT, layer0)
            dve.wait_ge(shared_in, 48)
            v.tensor_reduce(peak[:, 0, 1:4], w32[:, :, SHARED], AX.X, ALU.max,
                            apply_absolute_value=True).then_inc(peaks_a, 1)
            dve.wait_ge(peaks_a, NT + 1)
            v.tensor_reduce(peak[:, 0, 0:1], tile_peak[:], AX.X, ALU.max).then_inc(peaks_a, 1)
            dve.wait_ge(rows_ps, 1)
            dve.wait_ge(maps_ready, 1)
            v.tensor_copy(row_z, ps_misc[0:1, 0, 0:SLOTS])
            v.scalar_tensor_tensor(row_a, ps_misc[0:1, 1, 0:SLOTS], -1.0, land_id, ALU.mult, ALU.add)
            v.tensor_copy(w_slot, ps_down[:, 1, 0:SLOTS]).then_inc(rows_out, 1)

            def scales(which, done):
                pk, pw, ip, sc, wk = (a[:, which] for a in (peak_all, p2, ip2, scale, work))
                link(v.tensor_scalar(pk, pk, TINY, None, ALU.max))
                link(v.tensor_scalar(pw.bitcast(I32), pk.bitcast(I32), EXPONENT_MASK, None,
                                     ALU.bitwise_and))
                link(v.reciprocal(ip, pw))
                v.tensor_scalar(sc, ip, 2.0 ** TOP, None, ALU.mult)
                link(v.scalar_tensor_tensor(wk[:, 0:1], pw[:, 0:1], 2.0 ** (-2 * TOP), pw[:, 1:2],
                                            ALU.mult, ALU.mult))
                v.tensor_copy(g_scale[:, which:which + 1], wk[:, 0:1])
                link(v.scalar_tensor_tensor(u_scale[:, which:which + 1], ip[:, 0:1],
                                            2.0 ** (-2 * TOP - 3), ip[:, 1:2], ALU.mult, ALU.mult))
                link(v.scalar_tensor_tensor(wk[:, 1:2], pw[:, 0:1], 2.0 ** (3 - TOP), pw[:, 3:4],
                                            ALU.mult, ALU.mult))
                link(v.tensor_tensor(wk[:, 2:3], pw[:, 0:1], pw[:, 2:3], ALU.mult))
                link(v.tensor_tensor(wk[:, 3:4], wk[:, 2:3], pw[:, 1:2], ALU.mult))
                link(v.tensor_tensor(y_scale[:, which:which + 1], wk[:, 1:2], wk[:, 3:4], ALU.mult))
                link(v.reciprocal(y_unit[:, which:which + 1], y_scale[:, which:which + 1]))
                v.tensor_copy(wk[:, 4:5], y_unit[:, which:which + 1]).then_inc(done, 1)

            dve.wait_ge(peaks_all_a, 1)
            scales(0, scale_a)

            def lo(dst, src, s, hi, done):
                v.scalar_tensor_tensor(dst, src, s, hi, ALU.mult, ALU.subtract).then_inc(done, 1)

            def x_lo(t):
                b = ds(t * TB, TB)
                dve.wait_ge(x1_hi, t + 1)
                lo(x1s[:, b, 1], x1t[:, ds(t * TILE, TILE)].rearrange("p (b s) -> p b s", s=S),
                   scale[:, 0, 0:1], x1s[:, b, 0], x1_lo)

            def w_lo(kind, e, which, done):
                lo(w16[:, kind, ds(e * WSTRIDE + F, F)],
                   w32[:, kind, ds(e, 1)].rearrange("p u f -> p (u f)"),
                   scale[:, which, kind + 1:kind + 2], w16[:, kind, ds(e * WSTRIDE, F)], done)

            dve.wait_ge(ws_hi, 1)
            w_lo(0, SHARED, 0, ws_lo)
            x_lo(0)
            dve.wait_ge(ws_hi, 2)
            w_lo(1, SHARED, 0, ws_lo)
            dve.wait_ge(ws_hi, 3)
            w_lo(2, SHARED, 0, ws_lo)

            def hidden(st, k, c, width, which):
                dve.wait_ge(st.gelu[c], k + 1)
                dve.wait_ge(st.up[c], k + 1)
                first = isinstance(k, int) and k == 0
                if c >= 2:
                    dve.wait_ge(st.hidden_hi[c - 2], k + 1)
                    dve.wait_ge(st.hidden_lo[c - 2], k + 1)
                elif not first:
                    dve.wait_ge(st.hidden_hi[CHUNKS + c - 2], k)
                    dve.wait_ge(st.hidden_lo[CHUNKS + c - 2], k)
                v.scalar_tensor_tensor(hid[:, c % 2, 0:width], ps_up[:, c % 2, 0:width],
                                       u_scale[:, which:which + 1], act_g[:, c % 2, 0:width],
                                       ALU.mult, ALU.mult).then_inc(st.hidden[c], 1)

            def hidden_lo(st, k, c, par, width):
                dve.wait_ge(st.hidden_hi[c], k + 1)
                v.tensor_tensor(hid_lo[:, par, c, 0:width], hid[:, c % 2, 0:width],
                                hid_hi[:, par, c, 0:width], ALU.subtract
                                ).then_inc(st.hidden_lo[c], 1)

            def stage_start(prev):
                for c in range(CHUNKS - 2, CHUNKS):
                    dve.wait_ge(prev.hidden_hi[c], prev.n)
                    dve.wait_ge(prev.hidden_lo[c], prev.n)

            def take_base(k, par):
                dve.wait_ge(stage_a.down, k + 1)
                v.tensor_scalar(base[:, ds(k, 1)].rearrange("p u n -> p (u n)"), ps_down[:, par],
                                y_scale[:, 0:1], None, ALU.mult).then_inc(stage_a.taken, 1)

            def x1_in_units(k, par):
                if k >= 2:
                    dve.wait_ge(stage_a.down, k - 1)
                v.tensor_scalar(x1_unit[:, par], x1t[:, k * TILE:k * TILE + TILE], y_unit[:, 0:1],
                                None, ALU.mult).then_inc(x1_unit_a, 1)

            def experts_peaks():
                dve.wait_ge(down_squares, 1)
                root = peak[:, 1, 3:4].bitcast(I32)
                link(v.tensor_scalar(root, tmp_c[:, 15:16].bitcast(I32), 1, None,
                                     ALU.arith_shift_right))
                v.tensor_scalar(root, root, float(127 << 22), None, ALU.add)
                dve.wait_ge(gate_in, 16)
                dve.wait_ge(up_in, 16)
                for kind in (1, 0):
                    v.tensor_reduce(peak[:, 1, kind + 1:kind + 2],
                                    w32[:, kind, 0:E].rearrange("p e f -> p (e f)"), AX.X,
                                    ALU.max, apply_absolute_value=True)
                v.tensor_copy(peak[:, 1, 0:1], peak_all[:, 0, 0:1]).then_inc(peaks_b, 1)

            def slot_tables():
                link(v.tensor_scalar(row_c, row_z, 512.0, None, ALU.add))
                link(v.scalar_tensor_tensor(row_c, row_z, 0.0, row_c, ALU.is_lt, ALU.mult))
                link(v.scalar_tensor_tensor(row_a, row_z, 0.0, row_a, ALU.is_ge, ALU.mult))
                link(v.tensor_tensor(row_c, row_c, row_a, ALU.add))
                link(v.tensor_copy(dst_i[:], row_c))
                v.tensor_scalar(src_i[:], dst_i[:], B - 1, None, ALU.bitwise_and).then_inc(dst_row, 1)
                v.tensor_scalar(token_i[:], token_i[:], S - 1, None, ALU.bitwise_and)

            def token_table():
                dve.wait_ge(dst_all, 1)
                cols = tmp_cols.rearrange("p (k j) -> p k j", j=QB)
                link(v.tensor_tensor(
                    cols, ps_misc[:, 0, 0:SLOTS].rearrange("p (k s) -> p k s", s=GROUP)[:, :, SP_SLOTS:],
                    quarter[:].rearrange("p (u j) -> p u j", u=1).broadcast_to([P, BLOCKS, QB]),
                    ALU.mult))
                link(v.tensor_reduce(tmp_cols2, cols, AX.X, ALU.add))
                link(v.tensor_scalar(tmp_cols2, tmp_cols2, float(S), None, ALU.mult))
                link(v.tensor_tensor(dst_token[:], tmp_cols2, token_i[:].broadcast_to([P, BLOCKS]),
                                     ALU.add))

            def block_tables():
                link(v.tensor_tensor(cmp_b, block_slot[:], ends[0:1, 0:E - 1].rearrange(
                    "p (u e) -> p u e", u=1).broadcast_to([1, BLOCKS, E - 1]), ALU.is_ge))
                link(v.tensor_reduce(exp_f[:], cmp_b, AX.X, ALU.add))
                link(v.tensor_scalar(exp_i[:], exp_f[:], float(WSTRIDE), None, ALU.mult))
                link(v.tensor_tensor(
                    w_slot.rearrange("p (n j) -> p n j", j=QB),
                    w_slot.rearrange("p (n j) -> p n j", j=QB),
                    quarter[:].rearrange("p (u j) -> p u j", u=1).broadcast_to([P, BLOCKS * GQ, QB]),
                    ALU.mult))
                link(v.tensor_reduce(slot_w[:], w_slot.rearrange("p (n j) -> p n j", j=QB), AX.X,
                                     ALU.add))

            UNITS = FIRST * CHUNKS
            for k in range(FIRST):
                par = (stage_a.parity + k) % 2
                for c in range(CHUNKS):
                    n = k * CHUNKS + c
                    hidden(stage_a, k, c, TILE, 0)
                    if n == 0:
                        experts_peaks()
                    if n == 1:
                        x_lo(1)
                        dve.wait_ge(peaks_all_b, 1)
                        scales(1, scale_b)
                    if n == 2:
                        dve.wait_ge(maps_ready, 1)
                        slot_tables()
                    if n == 3:
                        x_lo(2)
                        block_tables()
                        token_table()
                        v.tensor_scalar(slot_w[:], slot_w[:], y_scale[:, 1:2], None, ALU.mult
                                        ).then_inc(routed, 1)
                    if c == 0 and k >= 2:
                        take_base(k - 2, par)
                    if c == 1:
                        x1_in_units(k, par)
                    if n >= 5:
                        mine = share(3 * E, n - 5, UNITS - 5)
                        dve.wait_ge(we_hi, mine.stop)
                        for i in mine:
                            w_lo(i % 3, i // 3, 1, we_lo)

            def take_block(k, j, par):
                dve.wait_ge(stage_b.down, k + 1)
                if not isinstance(k, int) or k >= 2:
                    dve.wait_ge(scattered[j], (k - j) * (8 * SP_SLOTS))
                    dve.wait_ge(group_scattered[j], (k - j) * 8)
                v.tensor_tensor(y_sb[:, j], ps_down[:, par, 0:GW].rearrange(
                    "p (q c) -> p q c", q=GQ), slot_w[:, ds(k * GQ, GQ)].rearrange(
                        "p (q u) -> p q u", u=1).broadcast_to([P, GQ, C]), ALU.mult
                    ).then_inc(stage_b.taken, 1)

            stage_start(stage_a)

            def expert_block(k, j):
                par = (stage_b.parity + j) % 2
                for c in range(CHUNKS):
                    hidden(stage_b, k, c, GW, 1)
                    if c >= 1:
                        hidden_lo(stage_b, k, c - 1, par, GW)
                    elif isinstance(k, int) and k < 2:
                        take_base(FIRST - 2 + k, par)
                    else:
                        take_block(k - 2, j, par)
                hidden_lo(stage_b, k, CHUNKS - 1, par, GW)
            steps(dve, BLOCKS, expert_block, 4)

            def take_out(k, par):
                dve.wait_ge(stage_c.down, k + 1)
                dve.wait_ge(back_sum, k + 1)
                tile = back[:, FIRST + k, 0]
                v.scalar_tensor_tensor(tile, ps_down[:, par], y_scale[:, 0:1], tile, ALU.mult,
                                       ALU.add).then_inc(finished, 1)

            stage_start(stage_b)
            for k in range(LATER):
                par = (stage_c.parity + k) % 2
                for c in range(CHUNKS):
                    hidden(stage_c, k, c, TILE, 0)
                    if c >= 1:
                        hidden_lo(stage_c, k, c - 1, par, TILE)
                    if k == 0 and c in (0, 2):
                        b = BLOCKS - 2 + c // 2
                        take_block(b, b % 2, (stage_b.parity + b) % 2)
                    if k >= 2 and c == 2:
                        take_out(k - 2, par)
                hidden_lo(stage_c, k, CHUNKS - 1, par, TILE)
            for t in range(FIRST):
                dve.wait_ge(back_sum, LATER + t + 1)
                v.tensor_tensor(base[:, t], base[:, t], back[:, t, 0], ALU.add
                                ).then_inc(finished, 1)
            for k in range(LATER - 2, LATER):
                take_out(k, (stage_c.parity + k) % 2)

        @block.gpsimd
        def _(pool):
            g = nc.gpsimd
            chain = [0]

            def link(ins):
                chain[0] += 1
                ins.then_inc(pool_chain, 1)
                pool.wait_ge(pool_chain, chain[0])

            link(g.memset(ident[:], 0.0))
            g.affine_select(out=ident[:], in_=ident[:], compare_op=ALU.not_equal, fill=1.0, base=0,
                            pattern=[[-1, P]], channel_multiplier=1)
            link(g.memset(adapter_rows[:], 1.0))
            link(g.affine_select(out=adapter_rows[:], in_=adapter_rows[:], compare_op=ALU.is_ge,
                                 fill=0.0, base=0, pattern=[[1, P]], channel_multiplier=-R))
            g.affine_select(out=adapter_rows[:], in_=adapter_rows[:], compare_op=ALU.is_ge, fill=0.0,
                            base=R - 1, pattern=[[-1, P]], channel_multiplier=R).then_inc(consts, 1)
            iota = dict(allow_small_or_imprecise_dtypes=True, channel_multiplier=0)
            g.iota(rev[:], pattern=[[-1, E]], base=E, **iota)
            g.iota(fills[:], pattern=[[0, E], [GROUP, FILLS]], base=0, **iota)
            link(g.memset(upto[:], float(GROUP)))
            g.affine_select(out=upto[:], in_=upto[:], compare_op=ALU.is_ge, fill=0.0, base=0,
                            pattern=[[1, E], [-1, E]], channel_multiplier=0)
            g.memset(ones[:], 1.0).then_inc(consts, 1)
            link(g.memset(before_me[:], 1.0))
            g.affine_select(out=before_me[:], in_=before_me[:], compare_op=ALU.is_gt, fill=0.0, base=0,
                            pattern=[[1, P]], channel_multiplier=-1).then_inc(consts2, 1)
            g.iota(token_i[:], pattern=[[0, 1]], base=0, channel_multiplier=1)
            g.memset(ones_h[:], 1.0)
            g.memset(b128_h[:], float(B))
            g.iota(batch_m512[:], pattern=[[0, 1]], base=-512, channel_multiplier=1,
                   allow_small_or_imprecise_dtypes=True)
            g.iota(slot_id, pattern=[[1, SLOTS]], base=0, **iota)
            g.iota(land_id, pattern=[[1, SLOTS]], base=LAND, **iota)
            g.iota(block_slot[:], pattern=[[GROUP, BLOCKS], [0, E - 1]], base=0, **iota)
            link(g.memset(quarter[:], 1.0))
            link(g.affine_select(out=quarter[:], in_=quarter[:], compare_op=ALU.is_ge, fill=0.0, base=0,
                                 pattern=[[-S, QB]], channel_multiplier=1))
            link(g.affine_select(out=quarter[:], in_=quarter[:], compare_op=ALU.is_ge, fill=0.0,
                                 base=S - 1, pattern=[[S, QB]], channel_multiplier=-1))

            pool.wait_ge(pos_ready, 1)
            g.tensor_scalar(slot1, slot_id, pos[:, 0:1], None, ALU.is_equal)
            g.tensor_scalar(slot2, slot_id, pos[:, 1:2], None, ALU.is_equal)
            g.tensor_scalar(below_h[:, 0], slot_id, pos[:, 0:1], None, ALU.is_gt)
            link(g.tensor_scalar(below_h[:, 1], slot_id, pos[:, 1:2], None, ALU.is_gt))
            g.tensor_tensor(taken_h[:], slot1, slot2, ALU.add)
            g.tensor_copy(second_h[:], slot2)
            g.tensor_tensor(below_h[:, 0], below_h[:, 0], below_h[:, 1], ALU.add).then_inc(maps_ready, 1)

            pool.wait_ge(peaks_a, NT + 2)
            g.partition_all_reduce(peak_all[:, 0], peak[:, 0], P, ABSMAX).then_inc(peaks_all_a, 1)

            pool.wait_ge(scale_a, 1)
            UNITS = FIRST * CHUNKS
            XLO_UNITS = (3, 5, 7, 9, 11)

            def x_lo(t):
                pool.wait_ge(x1_lo, t)
                link(g.tensor_tensor(x_scaled, x1t[:, t * TILE:t * TILE + TILE],
                                     scale[:, 0, 0:1].broadcast_to([P, TILE]), ALU.mult))
                pool.wait_ge(x1_hi, t + 1)
                b = slice(t * TB, t * TB + TB)
                g.tensor_tensor(x1s[:, b, 1], x_scaled.rearrange("p (b s) -> p b s", s=S),
                                x1s[:, b, 0], ALU.subtract).then_inc(x1_lo, 1)

            def gather(k, par, first, count, taken=None):
                src = values(ET.Pool, src_i[0:1, ds(k * GROUP + first, count)], 0, B - 1)
                for i in range(count):
                    if i == count - 1 and taken is not None:
                        pool.wait_ge(stage_b.taken, taken + 1)
                    cp = g.tensor_copy(
                        gathered[:, par, first + i].rearrange("p h s -> p (h s)"),
                        x1s[:, ds(src[i], 1)].rearrange("p u h s -> p (u h s)"))
                if first + count == GROUP:
                    cp.then_inc(slots_in, 1)

            for k in range(FIRST):
                par = (stage_a.parity + k) % 2
                for c in range(CHUNKS):
                    n = k * CHUNKS + c
                    pool.wait_ge(stage_a.hidden_hi[c], k + 1)
                    g.tensor_tensor(hid_lo[:, par, c], hid[:, c % 2], hid_hi[:, par, c], ALU.subtract
                                    ).then_inc(stage_a.hidden_lo[c], 1)
                    if n == 0:
                        pool.wait_ge(peaks_b, 1)
                        g.partition_all_reduce(peak_all[:, 1], peak[:, 1], P, ABSMAX
                                               ).then_inc(peaks_all_b, 1)
                    if n in XLO_UNITS:
                        x_lo(3 + XLO_UNITS.index(n))
                    if n == UNITS - 4:
                        pool.wait_ge(routed, 1)
                        pool.wait_ge(x1_hi, NT)
                        pool.wait_ge(x1_lo, NT)
                    if UNITS - 4 <= n < UNITS - 1:
                        a = (n - UNITS + 4) * QB
                        gather(0, stage_b.parity, a, QB)

            def set_offsets(k, j):
                if not isinstance(k, int) or k >= 2:
                    pool.wait_ge(group_scattered[j], (k - j) * 8)
                g.tensor_copy(dst_now[:, j:j + 1], dst_token[:, ds(k, 1)]).then_inc(offsets_set, 1)
                pool.wait_ge(offsets_set, k + 1)

            def scatter(j):
                g.indirect_dma_start(
                    expert_out.rearrange("r s c -> (r s) c"),
                    bass.IndirectOffsetOnAxis(ap=dst_now[:, j:j + 1], axis=0),
                    y_sb[:, j, GQ - 1], None).then_inc(group_scattered[j], 16)

            def gather_block(k, j):
                if isinstance(k, int) and k < LAG:
                    if k >= 2:
                        pool.wait_ge(stage_b.up[CHUNKS - 1], k - 1)
                    if k > 0:
                        gather(k, (stage_b.parity + j) % 2, 0, GROUP)
                    return
                set_offsets(k - LAG, (j - LAG) % 2)
                pool.wait_ge(stage_b.up[CHUNKS - 1], k - 1)
                gather(k, (stage_b.parity + j) % 2, 0, GROUP, k - LAG)
                scatter((j - LAG) % 2)
            steps(pool, BLOCKS, gather_block, LAG + 3)
            for k in range(BLOCKS - LAG, BLOCKS):
                set_offsets(k, k % 2)
                pool.wait_ge(stage_b.taken, k + 1)
                scatter(k % 2)

            for t in FINALS:
                pool.wait_ge(back_in[t], 2 * 16)
                g.tensor_tensor(back[:, t, 0], back[:, t, 0], back[:, t, 1], ALU.add
                                ).then_inc(back_sum, 1)

    return nc


_INS = ["x", "cond_8", "L0_cond_W_base", "L0_cond_b_base", "L0_cond_As", "L0_cond_Bs",
        "L1_cond_skill_gate", "L1_cond_skill_up", "L1_cond_skill_down", "L1_cond_shared_gate",
        "L1_cond_shared_up", "L1_cond_shared_down"]
_OUT = ((128, 32, 128), "float32")


def kernel(**inputs):
    import numpy as _np
    import concourse.bacc as _bacc
    from concourse import mybir as _mybir
    from concourse.bass_utils import run_bass_kernel_spmd as _run

    nc = _bacc.Bacc("TRN2", target_bir_lowering=False, num_devices=1)
    arrays, args = {}, []
    for name in _INS:
        a = _np.ascontiguousarray(inputs[name])
        arrays[f"in_{name}"] = a
        args.append(nc.dram_tensor(f"in_{name}", a.shape, _mybir.dt.from_np(a.dtype),
                                   kind="ExternalInput").ap())
    out = nc.dram_tensor("out_0", _OUT[0], _mybir.dt.from_np(_np.dtype(_OUT[1])),
                         kind="ExternalOutput").ap()
    lora_moe_kernel(nc, *args, out)
    r = _run(nc, [arrays], core_ids=[0])
    return r.results[0]["out_0"]
```

```python
from contextlib import ExitStack

import concourse.bass as bass
from concourse import mybir

ALU = mybir.AluOpType
ACT = mybir.ActivationFunctionType
AX = mybir.AxisListType
ET = mybir.EngineType
F16 = mybir.dt.float16
F32 = mybir.dt.float32
I32 = mybir.dt.int32
ABSMAX = bass.bass_isa.ReduceOp.absmax
ds = bass.ds

P = 128
EXPONENT_MASK = 0x7F800000
TINY = 2.0 ** -24
TOP = 14
MASKED = -3.0e38


def ceil_div(a, b):
    return -(-a // b)


class Stage:

    def __init__(self, sem, name, n, chunks, parity):
        self.n, self.parity = n, parity
        self.last_parity = (parity + n - 1) % 2
        self.gate = [sem(f"{name}_gate_{c}") for c in range(chunks)]
        self.up = [sem(f"{name}_up_{c}") for c in range(chunks)]
        self.gelu = [sem(f"{name}_gelu_{c}") for c in range(chunks)]
        self.hidden = [sem(f"{name}_hidden_{c}") for c in range(chunks)]
        self.hidden_hi = [sem(f"{name}_hidden_hi_{c}") for c in range(chunks)]
        self.hidden_lo = [sem(f"{name}_hidden_lo_{c}") for c in range(chunks)]
        self.down = sem(f"{name}_down")
        self.taken = sem(f"{name}_taken")


def lora_moe_kernel(nc, x, cond, w_base, b_base, lora_a, lora_b, skill_gate, skill_up, skill_down,
                    shared_gate, shared_up, shared_down, out):
    B, S, C = x.shape
    E, R, _ = lora_a.shape
    F = shared_gate.shape[1]
    LORA_SCALING = 32.0 / R
    MOE_SCALE = 1.0 / 12
    assert B == P and C == P and E * R == P and E == 8 and P % S == 0

    TILE = 512
    TB = TILE // S
    NT = B * S // TILE
    SUB = TILE // P
    QB = P // S
    CHUNKS = F // P
    XRING = 4
    FIRST = 5
    LATER = NT - FIRST
    GROUP = 12
    GW = GROUP * S
    GQ = GW // P
    BLOCKS = (2 * B + E * (GROUP - 1)) // GROUP
    SLOTS = BLOCKS * GROUP
    FILLS = ceil_div(B, GROUP)
    LAND = 2 * B
    WSTRIDE = 2 * F
    SP_SLOTS = GROUP - QB
    LAG = 3
    SHARED = E
    HI_TILES = (5, 6, 8)
    PEAKS = (0, 0, 1, 3, 3, 3, 4, 2)
    SQUARES = (0, 0, 0, 0, 0, 1, 2, 5, 0)
    FINALS = list(range(FIRST, NT)) + list(range(FIRST))
    STORES, POOL_TILES = (5, 0, 1, 2, 6, 3, 4, 7), (3, 4)
    TURN_UNITS, COPY_UNITS = (1, 3, 5, 7, 10), (2, 4, 6, 8, 11)
    HI_AHEAD, HI_UNITS = 3, (1, 18)
    LO_AHEAD, LO_UNITS = 1, (3, 19)
    WARM_UP = 7
    assert sum(PEAKS) == 2 * E and sum(SQUARES) == E
    assert (FIRST, LATER) == (5, 3) and NT % XRING == 0 and GW % P == 0

    with ExitStack() as ctx:
        def sb(name, shape, dt):
            return ctx.enter_context(nc.sbuf_tensor(name, shape, dt))

        def psum(name, shape):
            return ctx.enter_context(nc.psum_tensor(name, shape, F32))

        def sem(name):
            return ctx.enter_context(nc.semaphore(name))

        expert_out = nc.dram_tensor("expert_out", [SLOTS, S, C], F32, kind="Internal").ap()

        ps_gate = psum("ps_gate", [P, 2, TILE])
        ps_up = psum("ps_up", [P, 2, TILE])
        ps_down = psum("ps_down", [P, 2, TILE])
        ps_misc = psum("ps_misc", [P, 2, TILE])
        ps_xt, ps_lora, ps_x1 = ps_gate, ps_up, ps_down

        ident = sb("ident", [P, P], F32)
        adapter_rows = sb("adapter_rows", [E, P], F32)
        before_me = sb("before_me", [P, P], F32)
        ones = sb("ones", [P, P], F32)
        ones_h = sb("ones_h", [P, 1], F16)
        batch_m512 = sb("batch_m512", [P, 1], F16)
        b128_h = sb("b128_h", [P, 1], F16)
        rev = sb("rev", [P, E], F32)
        fills = sb("fills", [P, E, FILLS], F32)
        upto = sb("upto", [P, E, E], F32)
        quarter = sb("quarter", [P, QB], F32)
        block_slot = sb("block_slot", [1, BLOCKS, E - 1], F32)

        cond_sb = sb("cond_sb", [P, E], F32)
        bias = sb("bias", [P, 1], F32)
        small_t = sb("small_t", [P, 3, P], F32)
        cond_t = sb("cond_t", [E, P], F32)
        lora_w = sb("lora_w", [P, B], F32)
        ring = sb("ring", [P, XRING, SUB, C], F32)
        xt = sb("xt", [P, 2, TILE], F32)
        x1t = sb("x1t", [P, B * S], F32)
        x1s = sb("x1s", [P, B, 2, S], F16)
        w32 = sb("w32", [P, 3, E + 1, F], F32)
        w16 = sb("w16", [P, 3, (E + 1) * WSTRIDE], F16)
        base = sb("base", [P, FIRST, TILE], F32)

        gate_e = sb("gate_e", [P, E], F32)
        choice = sb("choice", [P, 2, E], F32)
        tmp_e = sb("tmp_e", [P, 4, E], F32)
        tmp_c = sb("tmp_c", [P, 16], F32)
        chosen = sb("chosen", [P, E], F32)
        tmp_fill = sb("tmp_fill", [P, E, FILLS], F32)
        tmp_ee = sb("tmp_ee", [P, E, E], F32)
        n_blocks = sb("n_blocks", [P, E], F32)
        ends = sb("ends", [P, E], F32)
        place = sb("place", [P, E], F32)
        pos = sb("pos", [P, 2], F32)
        w_col = sb("w_col", [P, 2, P], F32)
        taken_h = sb("taken_h", [P, SLOTS], F16)
        second_h = sb("second_h", [P, SLOTS], F16)
        below_h = sb("below_h", [P, 2, SLOTS], F16)
        dst_i = sb("dst_i", [1, SLOTS], I32)
        src_i = sb("src_i", [1, SLOTS], I32)
        exp_f = sb("exp_f", [1, BLOCKS], F32)
        exp_i = sb("exp_i", [1, BLOCKS], I32)
        dst_token = sb("dst_token", [P, BLOCKS], I32)
        dst_now = sb("dst_now", [P, 2], I32)
        token_i = sb("token_i", [P, 1], I32)
        slot_w = sb("slot_w", [P, BLOCKS * GQ], F32)

        peak = sb("peak", [P, 2, 4], F32)
        peak_all = sb("peak_all", [P, 2, 4], F32)
        shared_scale = sb("shared_scale", [P, 4, 3], F32)
        squares = sb("squares", [P, E], F32)
        warm = sb("warm", [P, 1], F32)
        tile_peak = sb("tile_peak", [P, NT], F32)
        weight_peak = sb("weight_peak", [P, 2 * E], F32)
        p2 = sb("p2", [P, 2, 4], F32)
        ip2 = sb("ip2", [P, 2, 4], F32)
        scale = sb("scale", [P, 2, 4], F32)
        work = sb("work", [P, 2, 6], F32)
        g_scale = sb("g_scale", [P, 2], F32)
        u_scale = sb("u_scale", [P, 2], F32)
        y_scale = sb("y_scale", [P, 2], F32)

        act_g = sb("act_g", [P, 2, TILE], F32)
        hid = sb("hid", [P, 2, TILE], F32)
        hid_hi = sb("hid_hi", [P, 2, CHUNKS, TILE], F16)
        hid_lo = sb("hid_lo", [P, 2, CHUNKS, TILE], F16)
        gathered = sb("gathered", [P, 2, GROUP, 2, S], F16)
        y_sb = sb("y_sb", [P, 2, GQ, C], F32)

        slot1 = hid[:, 0, 0:SLOTS]
        slot2 = hid[:, 1, 0:SLOTS]
        back = w32[:].rearrange("p a e f -> p (a e f)")[:, 0:NT * 2 * TILE].rearrange(
            "p (t h n) -> p t h n", h=2, n=TILE)
        x_scaled = y_sb[:].rearrange("p j q c -> p (j q c)")[:, 0:TILE]
        wb_sb, la_sb, lb_sb = (base[:, 2, i * P:i * P + P] for i in range(3))
        mixed = base[:, 0:2]
        slot_id = act_g[:, 0, 0:SLOTS]
        land_id = act_g[0:1, 1, 0:SLOTS]
        spare = ring[:].rearrange("p t q c -> p (t q c)")
        row_z, row_a, row_c = (spare[0:1, i * SLOTS:(i + 1) * SLOTS] for i in range(3))
        w_slot = spare[:, 3 * SLOTS:4 * SLOTS]
        tmp_cols = spare[:, 5 * SLOTS:5 * SLOTS + BLOCKS * QB]
        tmp_cols2 = spare[:, 5 * SLOTS + BLOCKS * QB:5 * SLOTS + BLOCKS * (QB + 1)]
        cmp_b = spare[0:1, 4 * SLOTS:4 * SLOTS + BLOCKS * (E - 1)].rearrange(
            "p (k e) -> p k e", e=E - 1)

        cond_in, wa_in, lb_in, bias_in = sem("cond_in"), sem("wa_in"), sem("lb_in"), sem("bias_in")
        x_in = [sem(f"x_in_{i}") for i in range(XRING)]
        shared_in = sem("shared_in")
        gate_in, up_in = sem("gate_in"), sem("up_in")
        down_in = [sem("down_in_0"), sem("down_in_1")]
        consts = sem("consts")
        pool_chain, dve_chain, act_chain = sem("pool_chain"), sem("dve_chain"), sem("act_chain")
        w_tr, w_out, a_tr, a_out, b_tr, b_out = (
            sem("w_tr"), sem("w_out"), sem("a_tr"), sem("a_out"), sem("b_tr"), sem("b_out"))
        lora_w_ps, lora_w_ready = sem("lora_w_ps"), sem("lora_w_ready")
        neg_max, exped, chosen_ready, ranks, pos_ready, w_col_ready = (
            sem("neg_max"), sem("exped"), sem("chosen_ready"), sem("ranks"), sem("pos_ready"),
            sem("w_col_ready"))
        maps_ready, rows_ps, rows_out, routed = (
            sem("maps_ready"), sem("rows_ps"), sem("rows_out"), sem("routed"))
        dst_row, dst_all, offsets_set = sem("dst_row"), sem("dst_all"), sem("offsets_set")
        xt_ps, xt_out, lora_ps, lora_mixed, x1_ps, x1_out = (
            sem("xt_ps"), sem("xt_out"), sem("lora_ps"), sem("lora_mixed"), sem("x1_ps"),
            sem("x1_out"))
        peaks_s, peaks_all_s, scale_s_ready = sem("peaks_s"), sem("peaks_all_s"), sem("scale_s_ready")
        tile_peaks, peaks, peaks_all, scale_ready, units_ready = (
            sem("tile_peaks"), sem("peaks"), sem("peaks_all"), sem("scale_ready"),
            sem("units_ready"))
        down_squares = sem("down_squares")
        x1_hi, x1_lo = sem("x1_hi"), sem("x1_lo")
        ws_hi, ws_lo, we_hi, we_lo = sem("ws_hi"), sem("ws_lo"), sem("we_hi"), sem("we_lo")
        base_tr, base_out, later_tr = sem("base_tr"), sem("base_out"), sem("later_tr")
        slots_in, scattered = sem("slots_in"), [sem("scattered_0"), sem("scattered_1")]
        group_scattered = [sem("group_scattered_0"), sem("group_scattered_1")]
        back_in = [sem(f"back_in_{t}") for t in range(NT)]
        back_sum, finished, finished_by_pool, stored = (
            sem("back_sum"), sem("finished"), sem("finished_by_pool"), sem("stored"))
        stage_a = Stage(sem, "first", FIRST, CHUNKS, 0)
        stage_b = Stage(sem, "block", BLOCKS, CHUNKS, (stage_a.last_parity + 1) % 2)
        stage_c = Stage(sem, "later", LATER, CHUNKS, (stage_b.last_parity + 1) % 2)

        x_dram = x.rearrange("b s c -> (b s) c").rearrange("(t p q) c -> t p q c", q=SUB, p=P)
        out_dram = out.rearrange("b s c -> (b s) c").rearrange("(t p q) c -> t p q c", q=SUB, p=P)
        rows_dram = expert_out[0:2 * B].rearrange("r s c -> (r s) c").rearrange(
            "(t p q) c -> t p q c", q=SUB, p=P)

        def values(engine, ap, least, most):
            _, v = nc.values_load_multi_w_load_instructions(
                ap, engines=[engine], min_val=least, max_val=most,
                skip_runtime_bounds_check_because="the routing gives values in these bounds")
            return v

        def steps(e, n, step, peel=2):
            for k in range(peel):
                step(k, k % 2)
            turns = (n - peel) // 2
            with e.Fori(peel, peel + 2 * turns - 1, 2) as k:
                step(k, 0)
                step(k + 1, 1)
            if n % 2:
                step(n - 1, 0)

        def in_token_order(x):
            return x.rearrange("f (p q) -> f q p", q=SUB)

        def in_chunks(x, kind):
            return (x.rearrange("p (c m) -> p c m", c=CHUNKS) if kind == 2 else
                    x.rearrange("p (m c) -> p c m", c=CHUNKS))

        def half(kind, e, lo):
            a = e * WSTRIDE + lo * F
            return w16[:, kind, a:a + F].rearrange("p (c m) -> p c m", c=CHUNKS)

        def splits(unit, ahead, units):
            if not units[0] <= unit < units[1]:
                return range(0)
            r = share(3 * E - ahead, unit - units[0], units[1] - units[0])
            return range(ahead + r.start, ahead + r.stop)

        def share(n, i, of):
            return range(n * i // of, n * (i + 1) // of)

        block = ctx.enter_context(nc.Block())

        @block.sync
        def _(sp):
            sp.dma_start(cond_sb[:], cond).then_inc(cond_in, 16)
            sp.dma_start(wb_sb, w_base).then_inc(wa_in, 16)
            sp.dma_start(la_sb, lora_a.rearrange("e r c -> (e r) c")).then_inc(wa_in, 16)
            sp.dma_start(ring[:, 0], x_dram[0]).then_inc(x_in[0], 16)
            sp.dma_start(lb_sb.rearrange("o (e r) -> o e r", e=E), lora_b.rearrange("e o r -> o e r")
                         ).then_inc(lb_in, 16)
            sp.dma_start(bias[:], b_base.rearrange("(o u) -> o u", u=1)).then_inc(bias_in, 16)
            sp.dma_start(ring[:, 1], x_dram[1]).then_inc(x_in[1], 16)
            sp.dma_start(w32[:, 0, SHARED], shared_gate).then_inc(shared_in, 16)
            sp.dma_start(w32[:, 1, SHARED], shared_up).then_inc(shared_in, 16)
            sp.dma_start(ring[:, 2], x_dram[2]).then_inc(x_in[2], 16)
            sp.dma_start(w32[:, 2, SHARED].rearrange("p (c h) -> p c h", c=CHUNKS),
                         shared_down.rearrange("(p c) h -> p c h", p=P)).then_inc(shared_in, 16)
            sp.dma_start(ring[:, 3], x_dram[3]).then_inc(x_in[3], 16)
            sp.dma_start(w32[:, 0, 0:E], skill_gate.rearrange("e h i -> h e i")).then_inc(gate_in, 16)
            for t in range(XRING, NT):
                sp.wait_ge(xt_ps, t - XRING + 1)
                sp.dma_start(ring[:, t % XRING], x_dram[t]).then_inc(x_in[t % XRING], 16)
                if t == XRING:
                    sp.dma_start(w32[:, 1, 0:E], skill_up.rearrange("e h i -> h e i")
                                 ).then_inc(up_in, 16)
                if t >= NT - 2:
                    h = ds((t - NT + 2) * (E // 2), E // 2)
                    sp.dma_start(w32[:, 2, h].rearrange("p e (c h) -> p e c h", c=CHUNKS),
                                 skill_down[h].rearrange("e (p c) h -> p e c h", p=P)
                                 ).then_inc(down_in[t - NT + 2], 16)

            sp.wait_ge(routed, 1)

            def scatter(k, j):
                rows = values(ET.SP, dst_i[0:1, ds(k * GROUP, SP_SLOTS)], 0, SLOTS - 1)
                sp.wait_ge(stage_b.taken, k + 1)
                for i in range(SP_SLOTS):
                    part = i % QB * S
                    sp.dma_start(expert_out[ds(rows[i], 1)].rearrange("u s c -> (u s) c"),
                                 y_sb[part:part + S, j, i // QB]).then_inc(scattered[j], 16)
            steps(sp, BLOCKS, scatter)

            for j in range(2):
                sp.wait_ge(scattered[j], 16 * SP_SLOTS * BLOCKS // 2)
                sp.wait_ge(group_scattered[j], 16 * BLOCKS // 2)
            for t in FINALS:
                for h in range(2):
                    sp.dma_start(back[:, t, h].rearrange("p (q c) -> p q c", q=SUB),
                                 rows_dram[h * NT + t]).then_inc(back_in[t], 16)
            for n, t in enumerate(STORES):
                if t in POOL_TILES:
                    sp.wait_ge(finished_by_pool, POOL_TILES.index(t) + 1)
                else:
                    sp.wait_ge(finished, len(set(STORES[:n + 1]) - set(POOL_TILES)))
                done = base[:, t] if t < FIRST else back[:, t, 0]
                sp.dma_start(out_dram[t], done.rearrange("p (q c) -> p q c", q=SUB)
                             ).then_inc(stored, 16)
            sp.wait_ge(stored, 16 * NT)

        @block.tensor
        def _(pe):
            def turn(t):
                pe.wait_ge(x_in[t % XRING], 16 * (t // XRING + 1))
                if t >= 2:
                    pe.wait_ge(xt_out, t - 1)
                for q in range(SUB):
                    mm = pe.transpose(ps_xt[:, t % 2, q * P:q * P + P], ring[:, t % XRING, q],
                                      ident[:])
                mm.then_inc(xt_ps, 1)

            pe.wait_ge(consts, 1)
            for _ in range(WARM_UP):
                pe.matmul(ps_misc[:, 0, 0:P], ones[:], ones[:], start=True, stop=True)
            pe.wait_ge(consts, 2)
            pe.wait_ge(wa_in, 2 * 16)
            pe.transpose(ps_misc[:, 1, 0:P], wb_sb, ident[:]).then_inc(w_tr, 1)
            pe.transpose(ps_misc[:, 0, 0:P], la_sb, ident[:])
            pe.wait_ge(cond_in, 16)
            pe.transpose(ps_misc[0:E, 0, P:2 * P], cond_sb[:], ident[:]).then_inc(a_tr, 1)
            turn(0)
            pe.wait_ge(a_out, 1)
            pe.wait_ge(w_out, 1)
            pe.matmul(ps_misc[:, 1, 0:B], adapter_rows[:], cond_t[:], start=True, stop=True
                      ).then_inc(lora_w_ps, 1)
            for t in range(NT):
                pe.wait_ge(xt_out, t + 1)
                if t >= 2:
                    pe.wait_ge(x1_out, t - 1)
                pe.matmul(ps_lora[:, t % 2], small_t[:, 1], xt[:, t % 2], start=True, stop=True
                          ).then_inc(lora_ps, 1)
                pe.matmul(ps_x1[:, t % 2], small_t[:, 0], xt[:, t % 2], start=True, stop=False)
                if t == 0:
                    pe.wait_ge(lb_in, 16)
                    pe.transpose(ps_misc[:, 0, 0:P], lb_sb, ident[:]).then_inc(b_tr, 1)
                if t + 1 < NT:
                    turn(t + 1)
                if t == 0:
                    pe.wait_ge(b_out, 1)
                pe.wait_ge(lora_mixed, t + 1)
                pe.matmul(ps_x1[:, t % 2], small_t[:, 2], mixed[:, t % 2], start=False, stop=True
                          ).then_inc(x1_ps, 1)
                if t == 0:
                    pe.wait_ge(chosen_ready, 1)
                    pe.wait_ge(consts, 4)
                    pe.wait_ge(lora_w_ready, 1)
                    pe.matmul(ps_misc[:, 1, 0:E], before_me[:], chosen[:], start=True, stop=True)
                    pe.matmul(ps_misc[:, 1, E:2 * E], ones[:], chosen[:], start=True, stop=True
                              ).then_inc(ranks, 1)

            pe.wait_ge(maps_ready, 1)
            pe.wait_ge(pos_ready, 1)
            pe.wait_ge(w_col_ready, 1)
            pe.matmul(ps_misc[0:1, 0, 0:SLOTS], batch_m512[:], taken_h[:], start=True, stop=False)
            pe.matmul(ps_misc[0:1, 0, 0:SLOTS], b128_h[:], second_h[:], start=False, stop=True)
            pe.matmul(ps_misc[0:1, 1, 0:SLOTS], ones_h[:], below_h[:, 0], start=True, stop=True)
            pe.wait_ge(x1_out, NT)
            pe.matmul(ps_down[:, 1, 0:SLOTS], w_col[:, 0], slot1, start=True, stop=False)
            pe.matmul(ps_down[:, 1, 0:SLOTS], w_col[:, 1], slot2, start=False, stop=True
                      ).then_inc(rows_ps, 1)

            def gate_up(st, prev, k, c, weights, moving):
                x_hi, x_lo, width = moving
                for kind, bank, reads, last, done in (
                        (0, ps_gate, st.gelu, prev and prev.gelu, st.gate),
                        (1, ps_up, st.hidden, prev and prev.hidden, st.up)):
                    if c >= 2:
                        pe.wait_ge(reads[c - 2], k + 1)
                    elif not isinstance(k, int) or k > 0:
                        pe.wait_ge(reads[CHUNKS + c - 2], k)
                    elif prev is not None:
                        pe.wait_ge(last[CHUNKS + c - 2], prev.n)
                    w_hi, w_lo = weights(kind, c * P), weights(kind, F + c * P)
                    o = bank[:, c % 2, 0:width]
                    pe.matmul(o, w_hi, x_hi, start=True, stop=False)
                    pe.matmul(o, w_hi, x_lo, start=False, stop=False)
                    pe.matmul(o, w_lo, x_hi, start=False, stop=True).then_inc(done[c], 1)

            def wait_chunk(st, k, c):
                pe.wait_ge(st.hidden_hi[c], k + 1)
                pe.wait_ge(st.hidden_lo[c], k + 1)

            def block_down(k, par, c, weights):
                wait_chunk(stage_b, k, c)
                w_hi = weights(2, c * P)
                for q in range(GQ):
                    o, tokens = ps_down[:, par, q * P:q * P + P], slice(q * P, q * P + P)
                    pe.matmul(o, hid_hi[:, par, c, tokens], w_hi,
                              start=(c == 0 and q == 0), stop=False, skip_group_check=True)
                    pe.matmul(o, hid_lo[:, par, c, tokens], w_hi,
                              start=False, stop=False, skip_group_check=True)
                w_lo = weights(2, F + c * P)
                last = c == CHUNKS - 1
                for q in range(GQ):
                    mm = pe.matmul(ps_down[:, par, q * P:q * P + P],
                                   hid_hi[:, par, c, q * P:q * P + P], w_lo, start=False,
                                   stop=last, skip_group_check=True)
                if last:
                    mm.then_inc(stage_b.down, 1)

            def shared_weights(kind, at):
                a = SHARED * WSTRIDE + at
                return w16[:, kind, a:a + P]

            def expert_weights(offset):
                return lambda kind, at: w16[:, kind, at:][:, ds(offset, P)]

            def tile_moving(t):
                xs = x1s[:, t * TB:t * TB + TB]
                return xs[:, :, 0], xs[:, :, 1], TILE

            def block_moving(par):
                return gathered[:, par, :, 0], gathered[:, par, :, 1], GW

            def shared_down(st, k, par, c):
                wait_chunk(st, k, c)
                o, last = ps_down[:, par], c == CHUNKS - 1
                w_hi, w_lo = shared_weights(2, c * P), shared_weights(2, F + c * P)
                pe.matmul(o, w_hi, hid_hi[:, par, c], start=(c == 0), stop=False)
                pe.matmul(o, w_hi, hid_lo[:, par, c], start=False, stop=False)
                mm = pe.matmul(o, w_lo, hid_hi[:, par, c], start=False, stop=last)
                if last:
                    mm.then_inc(st.down, 1)

            def turn_back(t, bank, done):
                tile = in_token_order(x1t[:, t * TILE:t * TILE + TILE])
                for q in range(SUB):
                    mm = pe.transpose(bank[:, q * P:q * P + P], tile[:, q], ident[:])
                mm.then_inc(done, 1)

            pe.wait_ge(ws_hi, 2)
            pe.wait_ge(ws_lo, 2)

            for k in range(FIRST):
                par = (stage_a.parity + k) % 2
                pe.wait_ge(x1_hi, k + 1)
                pe.wait_ge(x1_lo, k + 1)
                for c in range(CHUNKS):
                    gate_up(stage_a, None, k, c, shared_weights, tile_moving(k))
                    if k == 1 and c == 0:
                        pe.wait_ge(rows_out, 1)
                        pe.wait_ge(ws_hi, 3)
                        pe.wait_ge(ws_lo, 3)
                    if k == 2 and c == 0:
                        pe.wait_ge(dst_row, 1)
                        pe.matmul(ps_misc[:, 0, 0:SLOTS], ones[0:1, :], row_c, start=True, stop=True
                                  ).then_inc(dst_all, 1)
                    if k > 0:
                        shared_down(stage_a, k - 1, 1 - par, c)

            pe.wait_ge(we_hi, 3 * E)
            pe.wait_ge(we_lo, 3 * E)
            pe.wait_ge(routed, 1)

            def expert_block(k, j):
                par = (stage_b.parity + j) % 2
                first = isinstance(k, int) and k == 0
                if first:
                    now = values(ET.PE, exp_i[0:1, 0:1], 0, (E - 1) * WSTRIDE)[0]
                else:
                    last, now = values(ET.PE, exp_i[0:1, ds(k - 1, 2)], 0, (E - 1) * WSTRIDE)
                pe.wait_ge(slots_in, k + 1)
                for c in range(CHUNKS):
                    gate_up(stage_b, stage_a, k, c, expert_weights(now), block_moving(par))
                    if first:
                        shared_down(stage_a, FIRST - 1, 1 - par, c)
                    else:
                        block_down(k - 1, 1 - par, c, expert_weights(last))
            steps(pe, BLOCKS, expert_block)

            last = values(ET.PE, exp_i[0:1, BLOCKS - 1:BLOCKS], 0, (E - 1) * WSTRIDE)[0]
            for k in range(LATER):
                par = (stage_c.parity + k) % 2
                for c in range(CHUNKS):
                    gate_up(stage_c, stage_b, k, c, shared_weights, tile_moving(k + FIRST))
                    if k > 0:
                        shared_down(stage_c, k - 1, 1 - par, c)
                    elif c < 2:
                        for d in (2 * c, 2 * c + 1):
                            block_down(BLOCKS - 1, 1 - par, d, expert_weights(last))
                    n = k * CHUNKS + c
                    if n in TURN_UNITS:
                        t = TURN_UNITS.index(n)
                        pe.wait_ge(stage_a.taken, t + 1)
                        if t > 0:
                            pe.wait_ge(base_out, t)
                        turn_back(t, ps_misc[:, 0], base_tr)
                    if n == 2 * CHUNKS + 1:
                        pe.wait_ge(stage_c.taken, 1)
                        turn_back(FIRST, ps_misc[:, 1], later_tr)
            pe.wait_ge(stage_c.gelu[2], LATER)
            pe.wait_ge(stage_c.gelu[3], LATER)
            for c in range(CHUNKS):
                shared_down(stage_c, LATER - 1, stage_c.last_parity, c)
                if c == 1:
                    pe.wait_ge(stage_c.taken, 2)
                    turn_back(FIRST + 1, ps_gate[:, 0], later_tr)
            pe.wait_ge(stage_c.taken, 3)
            turn_back(FIRST + 2, ps_gate[:, 1], later_tr)

        @block.scalar
        def _(act):
            act.wait_ge(neg_max, 1)
            nc.scalar.activation(gate_e[:], cond_sb[:], ACT.Exp, bias=tmp_c[:, 1:2]).then_inc(exped, 1)
            act.wait_ge(a_tr, 1)
            nc.scalar.activation(small_t[:, 1], ps_misc[:, 0, 0:P], ACT.Copy)
            nc.scalar.activation(cond_t[:], ps_misc[0:E, 0, P:2 * P], ACT.Copy).then_inc(a_out, 1)

            def split_hi(dst, src, s, done):
                nc.scalar.activation(dst, src, ACT.Copy, scale=s).then_inc(done, 1)

            def x_hi(t):
                split_hi(x1s[:, ds(t * TB, TB), 0], x1t[:, ds(t * TILE, TILE)].rearrange(
                    "p (b s) -> p b s", s=S), scale[:, 0, 0:1], x1_hi)

            def w_hi(i):
                e, kind = divmod(i, 3)
                split_hi(half(kind, e, 0), in_chunks(w32[:, kind, e], kind),
                         scale[:, 1, kind + 1:kind + 2], we_hi)

            for t in range(NT + 1):
                if t < NT:
                    act.wait_ge(xt_ps, t + 1)
                    if t >= 2:
                        act.wait_ge(x1_ps, t - 1)
                    nc.scalar.activation(in_token_order(xt[:, t % 2]),
                                         ps_xt[:, t % 2].rearrange("c (q p) -> c q p", q=SUB),
                                         ACT.Copy).then_inc(xt_out, 1)
                if t == 0:
                    act.wait_ge(b_tr, 1)
                    nc.scalar.activation(small_t[:, 2], ps_misc[:, 0, 0:P], ACT.Copy
                                         ).then_inc(b_out, 1)
                    act.wait_ge(bias_in, 16)
                else:
                    act.wait_ge(x1_ps, t)
                    nc.scalar.activation(x1t[:, (t - 1) * TILE:t * TILE], ps_x1[:, (t - 1) % 2],
                                         ACT.Identity, bias=bias[:, 0:1]).then_inc(x1_out, 1)
                if t in HI_TILES:
                    act.wait_ge(scale_s_ready, 1)
                    kind = HI_TILES.index(t)
                    split_hi(half(kind, SHARED, 0), in_chunks(w32[:, kind, SHARED], kind),
                             shared_scale[:, 3, kind:kind + 1], ws_hi)
                for e in range(sum(SQUARES[:t]), sum(SQUARES[:t + 1])):
                    act.wait_ge(down_in[e // (E // 2)], 16)
                    nc.scalar.activation(w16[:, 2, e * F:e * F + F], w32[:, 2, e], ACT.Square,
                                         accum_out=squares[:, e:e + 1]
                                         ).then_inc(down_squares, 1)
            nc.scalar.activation(warm[:], bias[:], ACT.Gelu_apprx_tanh)
            act.wait_ge(scale_ready, 1)
            x_hi(0)
            for i in range(HI_AHEAD):
                w_hi(i)

            def gelu(st, prev, k, c, width, which):
                act.wait_ge(st.gate[c], k + 1)
                first = isinstance(k, int) and k == 0
                if c >= 2:
                    act.wait_ge(st.hidden[c - 2], k + 1)
                elif not first:
                    act.wait_ge(st.hidden[CHUNKS + c - 2], k)
                elif prev is not None:
                    act.wait_ge(prev.hidden[CHUNKS + c - 2], prev.n)
                nc.scalar.activation(act_g[:, c % 2, 0:width], ps_gate[:, c % 2, 0:width],
                                     ACT.Gelu_apprx_tanh, scale=g_scale[:, which:which + 1]
                                     ).then_inc(st.gelu[c], 1)

            def hidden_hi(st, prev, k, c, par, width):
                act.wait_ge(st.hidden[c], k + 1)
                if c == 0:
                    if not isinstance(k, int) or k >= 2:
                        act.wait_ge(st.down, k - 1)
                    elif k == 0 and prev is not None:
                        act.wait_ge(prev.down, prev.n - 1)
                nc.scalar.activation(hid_hi[:, par, c, 0:width], hid[:, c % 2, 0:width], ACT.Copy
                                     ).then_inc(st.hidden_hi[c], 1)

            UNITS = FIRST * CHUNKS
            act.wait_ge(units_ready, 1)
            for k in range(FIRST):
                par = (stage_a.parity + k) % 2
                for c in range(CHUNKS):
                    n = k * CHUNKS + c
                    if n == 1:
                        act.wait_ge(rows_out, 1)
                    gelu(stage_a, None, k, c, TILE, 0)
                    if c >= 1:
                        hidden_hi(stage_a, None, k, c - 1, par, TILE)
                    if n % 2 == 0 and n // 2 + 1 < NT:
                        x_hi(n // 2 + 1)
                    for i in splits(n, HI_AHEAD, HI_UNITS):
                        w_hi(i)
                hidden_hi(stage_a, None, k, CHUNKS - 1, par, TILE)

            def expert_block(k, j):
                par = (stage_b.parity + j) % 2
                for c in range(CHUNKS):
                    gelu(stage_b, stage_a, k, c, GW, 1)
                    if c >= 1:
                        hidden_hi(stage_b, stage_a, k, c - 1, par, GW)
                hidden_hi(stage_b, stage_a, k, CHUNKS - 1, par, GW)
            steps(act, BLOCKS, expert_block, 4)

            for k in range(LATER):
                par = (stage_c.parity + k) % 2
                for c in range(CHUNKS):
                    gelu(stage_c, stage_b, k, c, TILE, 0)
                    if c >= 1:
                        hidden_hi(stage_c, stage_b, k, c - 1, par, TILE)
                    n = k * CHUNKS + c
                    if n in COPY_UNITS:
                        t = COPY_UNITS.index(n)
                        act.wait_ge(base_tr, t + 1)
                        nc.scalar.activation(base[:, t], ps_misc[:, 0], ACT.Copy).then_inc(base_out, 1)
                hidden_hi(stage_c, stage_b, k, CHUNKS - 1, par, TILE)

        @block.vector
        def _(dve):
            v = nc.vector
            chain = [0]

            def link(ins):
                chain[0] += 1
                ins.then_inc(dve_chain, 1)
                dve.wait_ge(dve_chain, chain[0])

            dve.wait_ge(cond_in, 16)
            link(v.tensor_reduce(tmp_c[:, 0:1], cond_sb[:], AX.X, ALU.max))
            v.tensor_scalar(tmp_c[:, 1:2], tmp_c[:, 0:1], -1.0, None, ALU.mult).then_inc(neg_max, 1)
            dve.wait_ge(consts, 3)
            link(v.scalar_tensor_tensor(tmp_e[:, 0], cond_sb[:], tmp_c[:, 0:1], rev[:], ALU.is_equal,
                                        ALU.mult))
            link(v.tensor_reduce(tmp_c[:, 2:3], tmp_e[:, 0], AX.X, ALU.max))
            link(v.tensor_scalar(choice[:, 0], rev[:], tmp_c[:, 2:3], None, ALU.is_equal))
            link(v.scalar_tensor_tensor(tmp_e[:, 1], choice[:, 0], MASKED, cond_sb[:], ALU.mult,
                                        ALU.add))
            link(v.tensor_reduce(tmp_c[:, 3:4], tmp_e[:, 1], AX.X, ALU.max))
            link(v.scalar_tensor_tensor(tmp_e[:, 0], tmp_e[:, 1], tmp_c[:, 3:4], rev[:],
                                        ALU.is_equal, ALU.mult))
            link(v.tensor_reduce(tmp_c[:, 4:5], tmp_e[:, 0], AX.X, ALU.max))
            link(v.tensor_scalar(choice[:, 1], rev[:], tmp_c[:, 4:5], None, ALU.is_equal))
            v.tensor_tensor(chosen[:], choice[:, 0], choice[:, 1], ALU.add).then_inc(chosen_ready, 1)

            def softmax():
                dve.wait_ge(exped, 1)
                link(v.tensor_reduce(tmp_c[:, 5:6], gate_e[:], AX.X, ALU.add))
                link(v.reciprocal(tmp_c[:, 6:7], tmp_c[:, 5:6]))
                link(v.tensor_scalar(tmp_e[:, 2], gate_e[:], tmp_c[:, 6:7], None, ALU.mult))
                link(v.tensor_tensor(tmp_e[:, 0:2], choice[:], tmp_e[:, 2:3].broadcast_to([P, 2, E]), ALU.mult))
                link(v.tensor_reduce(tmp_c[:, 7:9], tmp_e[:, 0:2], AX.X, ALU.add))
                link(v.tensor_reduce(tmp_c[:, 9:10], tmp_c[:, 7:9], AX.X, ALU.add))
                link(v.reciprocal(tmp_c[:, 10:11], tmp_c[:, 9:10]))
                link(v.tensor_scalar(tmp_c[:, 11:13], tmp_c[:, 7:9], tmp_c[:, 10:11], None, ALU.mult))
                link(v.tensor_scalar(tmp_c[:, 13:15], tmp_c[:, 11:13], MOE_SCALE, None, ALU.mult))
                link(v.scalar_tensor_tensor(tmp_c[:, 7:9], tmp_c[:, 11:13], 1.0 - MOE_SCALE,
                                            tmp_c[:, 13:15], ALU.mult, ALU.add))
                v.tensor_scalar(w_col[:, 0], ones[:], tmp_c[:, 7:8], None, ALU.mult)
                v.tensor_scalar(w_col[:, 1], ones[:], tmp_c[:, 8:9], None, ALU.mult).then_inc(w_col_ready, 1)

            def slots():
                dve.wait_ge(ranks, 1)
                link(v.tensor_copy(tmp_e[:, 0:2].rearrange("p a e -> p (a e)"), ps_misc[:, 1, 0:2 * E]))
                link(v.tensor_tensor(tmp_fill[:], tmp_e[:, 1].rearrange("p (e u) -> p e u", u=1)
                                     .broadcast_to([P, E, FILLS]), fills[:], ALU.is_gt))
                link(v.tensor_reduce(n_blocks[:], tmp_fill[:], AX.X, ALU.add))
                link(v.tensor_tensor(tmp_ee[:], n_blocks[:].rearrange("p (u e) -> p u e", u=1)
                                     .broadcast_to([P, E, E]), upto[:], ALU.mult))
                link(v.tensor_reduce(ends[:], tmp_ee[:], AX.X, ALU.add))
                link(v.scalar_tensor_tensor(tmp_e[:, 2], n_blocks[:], -float(GROUP), ends[:], ALU.mult,
                                            ALU.add))
                link(v.tensor_tensor(place[:], tmp_e[:, 0], tmp_e[:, 2], ALU.add))
                link(v.tensor_tensor(tmp_e[:, 0:2], choice[:], place[:].rearrange("p (u e) -> p u e", u=1)
                                     .broadcast_to([P, 2, E]), ALU.mult))
                v.tensor_reduce(pos[:], tmp_e[:, 0:2], AX.X, ALU.add).then_inc(pos_ready, 1)

            dve.wait_ge(w_tr, 1)
            v.tensor_tensor(small_t[:, 0], ps_misc[:, 1, 0:P], ident[:], ALU.add).then_inc(w_out, 1)
            dve.wait_ge(lora_w_ps, 1)
            v.tensor_scalar(lora_w[:], ps_misc[:, 1, 0:B], LORA_SCALING, None, ALU.mult
                            ).then_inc(lora_w_ready, 1)

            def peak_of(x, column):
                return v.tensor_reduce(column, x, AX.X, ALU.max, apply_absolute_value=True)

            def powers(pk, pw, ip, sc):
                link(v.tensor_scalar(pk, pk, TINY, None, ALU.max))
                link(v.tensor_scalar(pw.bitcast(I32), pk.bitcast(I32), EXPONENT_MASK, None,
                                     ALU.bitwise_and))
                link(v.reciprocal(ip, pw))
                return v.tensor_scalar(sc, ip, 2.0 ** TOP, None, ALU.mult)

            def tile_peak_of(t):
                dve.wait_ge(x1_out, t + 1)
                peak_of(x1t[:, t * TILE:t * TILE + TILE], tile_peak[:, t:t + 1]
                        ).then_inc(tile_peaks, 1)

            softmax()

            dve.wait_ge(lora_w_ready, 1)
            for t in range(NT):
                dve.wait_ge(lora_ps, t + 1)
                if t >= 2:
                    dve.wait_ge(x1_ps, t - 1)
                v.tensor_tensor(mixed[:, t % 2].rearrange("p (b s) -> p b s", s=S),
                                ps_lora[:, t % 2].rearrange("p (b s) -> p b s", s=S),
                                lora_w[:, t * TB:t * TB + TB].rearrange("p (b u) -> p b u", u=1)
                                .broadcast_to([P, TB, S]), ALU.mult).then_inc(lora_mixed, 1)
                if t >= 1:
                    tile_peak_of(t - 1)
                if t == 1:
                    slots()
                if t == 2:
                    dve.wait_ge(shared_in, 3 * 16)
                    peak_of(w32[:, :, SHARED], peak[:, 0, 1:4]).then_inc(peaks_s, 1)
                if t == 4:
                    dve.wait_ge(peaks_all_s, 1)
                    powers(*(shared_scale[:, i] for i in range(4))).then_inc(scale_s_ready, 1)
                for n in range(sum(PEAKS[:t]), sum(PEAKS[:t + 1])):
                    dve.wait_ge(gate_in if n < E else up_in, 16)
                    peak_of(w32[:, n // E, n % E], weight_peak[:, n:n + 1]).then_inc(tile_peaks, 1)
            dve.wait_ge(down_squares, E)
            link(v.tensor_reduce(tmp_c[:, 15:16], squares[:], AX.X, ALU.add))
            root = peak[:, 1, 3:4].bitcast(I32)
            link(v.tensor_scalar(root, tmp_c[:, 15:16].bitcast(I32), 1, None, ALU.arith_shift_right))
            link(v.tensor_scalar(root, root, float(127 << 22), None, ALU.add))
            dve.wait_ge(tile_peaks, NT - 1 + 2 * E)
            v.tensor_reduce(peak[:, 1, 1:3], weight_peak[:].rearrange("p (k e) -> p k e", e=E), AX.X,
                            ALU.max)
            tile_peak_of(NT - 1)
            dve.wait_ge(tile_peaks, NT + 2 * E)
            link(v.tensor_reduce(peak[:, 0, 0:1], tile_peak[:], AX.X, ALU.max))
            v.tensor_copy(peak[:, 1, 0:1], peak[:, 0, 0:1]).then_inc(peaks, 1)
            def scales():
                pw, ip = (lambda i: p2[:, :, i]), (lambda i: ip2[:, :, i])
                wk = [work[:, :, i] for i in range(4)]
                v.scalar_tensor_tensor(g_scale[:], pw(0), 2.0 ** (-2 * TOP), pw(1), ALU.mult, ALU.mult)
                v.scalar_tensor_tensor(u_scale[:], ip(0), 2.0 ** (-2 * TOP - 3), ip(1),
                                       ALU.mult, ALU.mult)
                v.scalar_tensor_tensor(wk[1], pw(0), 2.0 ** (3 - TOP), pw(3), ALU.mult, ALU.mult)
                link(v.tensor_tensor(wk[2], pw(0), pw(2), ALU.mult))
                link(v.tensor_tensor(wk[3], wk[2], pw(1), ALU.mult))
                return v.tensor_tensor(y_scale[:], wk[1], wk[3], ALU.mult)

            dve.wait_ge(peaks_all, 1)
            powers(*(a[:].rearrange("p w k -> p (w k)") for a in (peak_all, p2, ip2, scale))
                   ).then_inc(scale_ready, 1)
            dve.wait_ge(scale_ready, 1)
            def lo(dst, src, s, hi, done):
                v.scalar_tensor_tensor(dst, src, s, hi, ALU.mult, ALU.subtract).then_inc(done, 1)

            def x_lo(t):
                b = ds(t * TB, TB)
                dve.wait_ge(x1_hi, t + 1)
                lo(x1s[:, b, 1], x1t[:, ds(t * TILE, TILE)].rearrange("p (b s) -> p b s", s=S),
                   scale[:, 0, 0:1], x1s[:, b, 0], x1_lo)

            def w_lo(i):
                e, kind = divmod(i, 3)
                dve.wait_ge(we_hi, i + 1)
                lo(half(kind, e, 1), in_chunks(w32[:, kind, e], kind),
                   scale[:, 1, kind + 1:kind + 2], half(kind, e, 0), we_lo)

            x_lo(0)
            scales().then_inc(units_ready, 1)
            dve.wait_ge(units_ready, 1)
            dve.wait_ge(rows_ps, 1)
            dve.wait_ge(maps_ready, 1)
            v.tensor_copy(row_z, ps_misc[0:1, 0, 0:SLOTS])
            v.scalar_tensor_tensor(row_a, ps_misc[0:1, 1, 0:SLOTS], -1.0, land_id, ALU.mult, ALU.add)
            v.tensor_copy(w_slot, ps_down[:, 1, 0:SLOTS]).then_inc(rows_out, 1)
            for i in range(LO_AHEAD):
                w_lo(i)

            def hidden(st, k, c, width, which):
                dve.wait_ge(st.gelu[c], k + 1)
                dve.wait_ge(st.up[c], k + 1)
                first = isinstance(k, int) and k == 0
                if c >= 2:
                    dve.wait_ge(st.hidden_hi[c - 2], k + 1)
                    dve.wait_ge(st.hidden_lo[c - 2], k + 1)
                elif not first:
                    dve.wait_ge(st.hidden_hi[CHUNKS + c - 2], k)
                    dve.wait_ge(st.hidden_lo[CHUNKS + c - 2], k)
                v.scalar_tensor_tensor(hid[:, c % 2, 0:width], ps_up[:, c % 2, 0:width],
                                       u_scale[:, which:which + 1], act_g[:, c % 2, 0:width],
                                       ALU.mult, ALU.mult).then_inc(st.hidden[c], 1)

            def hidden_lo(st, k, c, par, width):
                dve.wait_ge(st.hidden_hi[c], k + 1)
                v.tensor_tensor(hid_lo[:, par, c, 0:width], hid[:, c % 2, 0:width],
                                hid_hi[:, par, c, 0:width], ALU.subtract
                                ).then_inc(st.hidden_lo[c], 1)

            def stage_start(prev):
                for c in range(CHUNKS - 2, CHUNKS):
                    dve.wait_ge(prev.hidden_hi[c], prev.n)
                    dve.wait_ge(prev.hidden_lo[c], prev.n)

            def take(st, k, t, par):
                dve.wait_ge(st.down, k + 1)
                tile = x1t[:, t * TILE:t * TILE + TILE]
                v.scalar_tensor_tensor(tile, ps_down[:, par], y_scale[:, 0:1], tile, ALU.mult,
                                       ALU.add).then_inc(st.taken, 1)

            def slot_rows():
                link(v.tensor_scalar(row_c, row_z, 512.0, None, ALU.add))
                link(v.scalar_tensor_tensor(row_c, row_z, 0.0, row_c, ALU.is_lt, ALU.mult))
                link(v.scalar_tensor_tensor(row_a, row_z, 0.0, row_a, ALU.is_ge, ALU.mult))

            def slot_batches():
                link(v.tensor_tensor(row_c, row_c, row_a, ALU.add))
                link(v.tensor_copy(dst_i[:], row_c))
                v.tensor_scalar(src_i[:], dst_i[:], B - 1, None, ALU.bitwise_and).then_inc(dst_row, 1)
                v.tensor_scalar(token_i[:], token_i[:], S - 1, None, ALU.bitwise_and)

            def block_experts():
                link(v.tensor_tensor(cmp_b, block_slot[:], ends[0:1, 0:E - 1].rearrange(
                    "p (u e) -> p u e", u=1).broadcast_to([1, BLOCKS, E - 1]), ALU.is_ge))
                link(v.tensor_reduce(exp_f[:], cmp_b, AX.X, ALU.add))
                v.tensor_scalar(exp_i[:], exp_f[:], float(WSTRIDE), None, ALU.mult)

            def token_weights():
                link(v.tensor_tensor(
                    w_slot.rearrange("p (n j) -> p n j", j=QB),
                    w_slot.rearrange("p (n j) -> p n j", j=QB),
                    quarter[:].rearrange("p (u j) -> p u j", u=1).broadcast_to([P, BLOCKS * GQ, QB]),
                    ALU.mult))
                link(v.tensor_reduce(slot_w[:], w_slot.rearrange("p (n j) -> p n j", j=QB), AX.X,
                                     ALU.add))
                link(v.tensor_scalar(slot_w[:], slot_w[:], y_scale[:, 1:2], None, ALU.mult))

            def token_rows():
                dve.wait_ge(dst_all, 1)
                cols = tmp_cols.rearrange("p (k j) -> p k j", j=QB)
                link(v.tensor_tensor(
                    cols, ps_misc[:, 0, 0:SLOTS].rearrange("p (k s) -> p k s", s=GROUP)[:, :, SP_SLOTS:],
                    quarter[:].rearrange("p (u j) -> p u j", u=1).broadcast_to([P, BLOCKS, QB]),
                    ALU.mult))
                link(v.tensor_reduce(tmp_cols2, cols, AX.X, ALU.add))
                link(v.tensor_scalar(tmp_cols2, tmp_cols2, float(S), None, ALU.mult))
                v.tensor_tensor(dst_token[:], tmp_cols2, token_i[:].broadcast_to([P, BLOCKS]),
                                ALU.add).then_inc(routed, 1)

            UNITS = FIRST * CHUNKS
            for k in range(FIRST):
                par = (stage_a.parity + k) % 2
                for c in range(CHUNKS):
                    n = k * CHUNKS + c
                    hidden(stage_a, k, c, TILE, 0)
                    if n in (1, 3):
                        x_lo(n // 2 + 1)
                    if n == 2:
                        slot_rows()
                    if n == 4:
                        slot_batches()
                    if n == 6:
                        block_experts()
                    if n == 8:
                        token_weights()
                    if n == 10:
                        token_rows()
                    if c == 0 and k >= 2:
                        take(stage_a, k - 2, k - 2, par)
                    for i in splits(n, LO_AHEAD, LO_UNITS):
                        w_lo(i)

            def take_block(k, j, par):
                dve.wait_ge(stage_b.down, k + 1)
                if not isinstance(k, int) or k >= 2:
                    dve.wait_ge(scattered[j], (k - j) * (8 * SP_SLOTS))
                    dve.wait_ge(group_scattered[j], (k - j) * 8)
                v.tensor_tensor(y_sb[:, j], ps_down[:, par, 0:GW].rearrange(
                    "p (q c) -> p q c", q=GQ), slot_w[:, ds(k * GQ, GQ)].rearrange(
                        "p (q u) -> p q u", u=1).broadcast_to([P, GQ, C]), ALU.mult
                    ).then_inc(stage_b.taken, 1)

            stage_start(stage_a)

            def expert_block(k, j):
                par = (stage_b.parity + j) % 2
                for c in range(CHUNKS):
                    hidden(stage_b, k, c, GW, 1)
                    if c >= 1:
                        hidden_lo(stage_b, k, c - 1, par, GW)
                    elif isinstance(k, int) and k < 2:
                        take(stage_a, FIRST - 2 + k, FIRST - 2 + k, par)
                    else:
                        take_block(k - 2, j, par)
                hidden_lo(stage_b, k, CHUNKS - 1, par, GW)
            steps(dve, BLOCKS, expert_block, 4)

            def finish(t):
                if t >= FIRST:
                    k = t - FIRST
                    dve.wait_ge(later_tr, k + 1)
                    dve.wait_ge(back_sum, k + 1)
                    bank = (ps_misc[:, 1], ps_gate[:, 0], ps_gate[:, 1])[k]
                    v.tensor_tensor(back[:, t, 0], bank, back[:, t, 0], ALU.add).then_inc(finished, 1)
                    return
                dve.wait_ge(base_out, t + 1)
                dve.wait_ge(back_sum, LATER + t + 1)
                v.tensor_tensor(base[:, t], base[:, t], back[:, t, 0], ALU.add).then_inc(finished, 1)

            stage_start(stage_b)
            for k in range(LATER):
                par = (stage_c.parity + k) % 2
                for c in range(CHUNKS):
                    hidden(stage_c, k, c, TILE, 0)
                    if c >= 1:
                        hidden_lo(stage_c, k, c - 1, par, TILE)
                    if k == 0 and c in (0, 2):
                        b = BLOCKS - 2 + c // 2
                        take_block(b, b % 2, (stage_b.parity + b) % 2)
                    if k == 2 and c == 0:
                        take(stage_c, 0, FIRST, par)
                    if k == 2 and c == 3:
                        finish(STORES[0])
                hidden_lo(stage_c, k, CHUNKS - 1, par, TILE)
            take(stage_c, 1, FIRST + 1, (stage_c.parity + 1) % 2)
            for t in (0, 1, 2, FIRST + 1):
                finish(t)
            take(stage_c, 2, FIRST + 2, stage_c.last_parity)
            finish(FIRST + 2)

        @block.gpsimd
        def _(pool):
            g = nc.gpsimd
            chain = [0]

            def link(ins):
                chain[0] += 1
                ins.then_inc(pool_chain, 1)
                pool.wait_ge(pool_chain, chain[0])

            g.memset(ones[:], 1.0).then_inc(consts, 1)
            link(g.memset(ident[:], 0.0))
            g.affine_select(out=ident[:], in_=ident[:], compare_op=ALU.not_equal, fill=1.0, base=0,
                            pattern=[[-1, P]], channel_multiplier=1)
            link(g.memset(adapter_rows[:], 1.0))
            link(g.affine_select(out=adapter_rows[:], in_=adapter_rows[:], compare_op=ALU.is_ge,
                                 fill=0.0, base=0, pattern=[[1, P]], channel_multiplier=-R))
            g.affine_select(out=adapter_rows[:], in_=adapter_rows[:], compare_op=ALU.is_ge, fill=0.0,
                            base=R - 1, pattern=[[-1, P]], channel_multiplier=R).then_inc(consts, 1)
            iota = dict(allow_small_or_imprecise_dtypes=True, channel_multiplier=0)
            g.iota(rev[:], pattern=[[-1, E]], base=E, **iota)
            g.iota(fills[:], pattern=[[0, E], [GROUP, FILLS]], base=0, **iota)
            link(g.memset(upto[:], float(GROUP)))
            g.affine_select(out=upto[:], in_=upto[:], compare_op=ALU.is_ge, fill=0.0, base=0,
                            pattern=[[1, E], [-1, E]], channel_multiplier=0).then_inc(consts, 1)
            link(g.memset(before_me[:], 1.0))
            g.affine_select(out=before_me[:], in_=before_me[:], compare_op=ALU.is_gt, fill=0.0, base=0,
                            pattern=[[1, P]], channel_multiplier=-1).then_inc(consts, 1)
            g.iota(token_i[:], pattern=[[0, 1]], base=0, channel_multiplier=1)
            g.memset(ones_h[:], 1.0)
            g.memset(b128_h[:], float(B))
            g.iota(batch_m512[:], pattern=[[0, 1]], base=-512, channel_multiplier=1,
                   allow_small_or_imprecise_dtypes=True)
            g.iota(slot_id, pattern=[[1, SLOTS]], base=0, **iota)
            g.iota(land_id, pattern=[[1, SLOTS]], base=LAND, **iota)
            g.iota(block_slot[:], pattern=[[GROUP, BLOCKS], [0, E - 1]], base=0, **iota)
            link(g.memset(quarter[:], 1.0))
            link(g.affine_select(out=quarter[:], in_=quarter[:], compare_op=ALU.is_ge, fill=0.0, base=0,
                                 pattern=[[-S, QB]], channel_multiplier=1))
            link(g.affine_select(out=quarter[:], in_=quarter[:], compare_op=ALU.is_ge, fill=0.0,
                                 base=S - 1, pattern=[[S, QB]], channel_multiplier=-1))

            pool.wait_ge(pos_ready, 1)
            g.tensor_scalar(slot1, slot_id, pos[:, 0:1], None, ALU.is_equal)
            g.tensor_scalar(slot2, slot_id, pos[:, 1:2], None, ALU.is_equal)
            g.tensor_scalar(below_h[:, 0], slot_id, pos[:, 0:1], None, ALU.is_gt)
            link(g.tensor_scalar(below_h[:, 1], slot_id, pos[:, 1:2], None, ALU.is_gt))
            pool.wait_ge(peaks_s, 1)
            g.partition_all_reduce(shared_scale[:, 0], peak[:, 0, 1:4], P, ABSMAX
                                   ).then_inc(peaks_all_s, 1)
            g.tensor_tensor(taken_h[:], slot1, slot2, ALU.add)
            g.tensor_copy(second_h[:], slot2)
            g.tensor_tensor(below_h[:, 0], below_h[:, 0], below_h[:, 1], ALU.add).then_inc(maps_ready, 1)

            pool.wait_ge(scale_s_ready, 1)
            def shared_lo(kind):
                if kind > 0:
                    pool.wait_ge(ws_lo, kind)
                link(g.tensor_tensor(x_scaled, w32[:, kind, SHARED],
                                     shared_scale[:, 3, kind:kind + 1].broadcast_to([P, F]), ALU.mult))
                pool.wait_ge(ws_hi, kind + 1)
                g.tensor_tensor(half(kind, SHARED, 1), in_chunks(x_scaled, kind),
                                half(kind, SHARED, 0), ALU.subtract).then_inc(ws_lo, 1)

            shared_lo(0)
            shared_lo(1)
            pool.wait_ge(peaks, 1)
            g.partition_all_reduce(peak_all[:].rearrange("p w k -> p (w k)"),
                                   peak[:].rearrange("p w k -> p (w k)"), P, ABSMAX
                                   ).then_inc(peaks_all, 1)
            shared_lo(2)

            pool.wait_ge(scale_ready, 1)
            UNITS = FIRST * CHUNKS
            XLO_UNITS = (3, 5, 7, 9, 11)

            def x_scale(t):
                pool.wait_ge(x1_lo, t)
                link(g.tensor_tensor(x_scaled, x1t[:, t * TILE:t * TILE + TILE],
                                     scale[:, 0, 0:1].broadcast_to([P, TILE]), ALU.mult))

            def x_lo(t):
                pool.wait_ge(x1_hi, t + 1)
                b = slice(t * TB, t * TB + TB)
                g.tensor_tensor(x1s[:, b, 1], x_scaled.rearrange("p (b s) -> p b s", s=S),
                                x1s[:, b, 0], ALU.subtract).then_inc(x1_lo, 1)

            def gather(k, par, first, count, taken=None):
                src = values(ET.Pool, src_i[0:1, ds(k * GROUP + first, count)], 0, B - 1)
                for i in range(count):
                    if i == count - 1 and taken is not None:
                        pool.wait_ge(stage_b.taken, taken + 1)
                    cp = g.tensor_copy(
                        gathered[:, par, first + i].rearrange("p h s -> p (h s)"),
                        x1s[:, ds(src[i], 1)].rearrange("p u h s -> p (u h s)"))
                if first + count == GROUP:
                    cp.then_inc(slots_in, 1)

            for k in range(FIRST):
                par = (stage_a.parity + k) % 2
                for c in range(CHUNKS):
                    n = k * CHUNKS + c
                    pool.wait_ge(stage_a.hidden_hi[c], k + 1)
                    g.tensor_tensor(hid_lo[:, par, c], hid[:, c % 2], hid_hi[:, par, c], ALU.subtract
                                    ).then_inc(stage_a.hidden_lo[c], 1)
                    if n in XLO_UNITS:
                        x_scale(3 + XLO_UNITS.index(n))
                    if n - 1 in XLO_UNITS:
                        x_lo(3 + XLO_UNITS.index(n - 1))
                    if n == UNITS - 6:
                        pool.wait_ge(routed, 1)
                        pool.wait_ge(x1_hi, NT)
                        pool.wait_ge(x1_lo, NT)
                    if UNITS - 6 <= n < UNITS - 2:
                        part = GROUP // 4
                        gather(0, stage_b.parity, (n - UNITS + 6) * part, part)

            def set_offsets(k, j):
                if not isinstance(k, int) or k >= 2:
                    pool.wait_ge(group_scattered[j], (k - j) * 8)
                g.tensor_copy(dst_now[:, j:j + 1], dst_token[:, ds(k, 1)]).then_inc(offsets_set, 1)
                pool.wait_ge(offsets_set, k + 1)

            def scatter(j):
                g.indirect_dma_start(
                    expert_out.rearrange("r s c -> (r s) c"),
                    bass.IndirectOffsetOnAxis(ap=dst_now[:, j:j + 1], axis=0),
                    y_sb[:, j, GQ - 1], None).then_inc(group_scattered[j], 16)

            def gather_block(k, j):
                if isinstance(k, int) and k < LAG:
                    if k >= 2:
                        pool.wait_ge(stage_b.up[CHUNKS - 1], k - 1)
                    if k > 0:
                        gather(k, (stage_b.parity + j) % 2, 0, GROUP)
                    return
                set_offsets(k - LAG, (j - LAG) % 2)
                pool.wait_ge(stage_b.up[CHUNKS - 1], k - 1)
                gather(k, (stage_b.parity + j) % 2, 0, GROUP, k - LAG)
                scatter((j - LAG) % 2)
            steps(pool, BLOCKS, gather_block, LAG + 3)
            for k in range(BLOCKS - LAG, BLOCKS):
                set_offsets(k, k % 2)
                pool.wait_ge(stage_b.taken, k + 1)
                scatter(k % 2)

            for t in FINALS:
                pool.wait_ge(back_in[t], 2 * 16)
                add = g.tensor_tensor(back[:, t, 0], back[:, t, 0], back[:, t, 1], ALU.add)
                if t in POOL_TILES:
                    link(add)
                    pool.wait_ge(base_out, t + 1)
                    g.tensor_tensor(base[:, t], base[:, t], back[:, t, 0], ALU.add
                                    ).then_inc(finished_by_pool, 1)
                else:
                    add.then_inc(back_sum, 1)

    return nc


_INS = ["x", "cond_8", "L0_cond_W_base", "L0_cond_b_base", "L0_cond_As", "L0_cond_Bs",
        "L1_cond_skill_gate", "L1_cond_skill_up", "L1_cond_skill_down", "L1_cond_shared_gate",
        "L1_cond_shared_up", "L1_cond_shared_down"]
_OUT = ((128, 32, 128), "float32")


def kernel(**inputs):
    import numpy as _np
    import concourse.bacc as _bacc
    from concourse import mybir as _mybir
    from concourse.bass_utils import run_bass_kernel_spmd as _run

    nc = _bacc.Bacc("TRN2", target_bir_lowering=False, num_devices=1)
    arrays, args = {}, []
    for name in _INS:
        a = _np.ascontiguousarray(inputs[name])
        arrays[f"in_{name}"] = a
        args.append(nc.dram_tensor(f"in_{name}", a.shape, _mybir.dt.from_np(a.dtype),
                                   kind="ExternalInput").ap())
    out = nc.dram_tensor("out_0", _OUT[0], _mybir.dt.from_np(_np.dtype(_OUT[1])),
                         kind="ExternalOutput").ap()
    lora_moe_kernel(nc, *args, out)
    r = _run(nc, [arrays], core_ids=[0])
    return r.results[0]["out_0"]
```
